# Optimizing a Trainium2 kernel written in Bass

```python
import numpy as np
import jax
import jax.numpy as jnp

def _softmax(x, axis=-1):
    return jax.nn.softmax(x, axis=axis)

def _gelu(x):
    return jax.nn.gelu(x, approximate=True)

def _silu(x):
    return jax.nn.silu(x)

def _sigmoid(x):
    return jax.nn.sigmoid(x)

def _layernorm(x, axis=-1, eps=1e-05):
    m = jnp.mean(x, axis=axis, keepdims=True)
    v = jnp.var(x, axis=axis, keepdims=True)
    return (x - m) / jnp.sqrt(v + eps)

def _scatter_add(tgt, idx, src, axis=0):
    return tgt.at[idx].add(src)

def _segment_sum(src, seg, n):
    return jax.ops.segment_sum(src, seg, n)
kernel_name = 'mk_seq_preln_d2_jaxref_r8_c6eacd'

def setup_inputs(seed: int=0):
    np.random.seed(seed)
    _w = jnp.asarray

    def _L0_attn_setup():
        import jax, jax.numpy as jnp
        import numpy as np
        D_MODEL, D_STATE, D_INNER = (128, 16, 256)
        B, S = (2, 512)
        EPS = 1e-05
        key = jax.random.key(seed)
        ks = jax.random.split(key, 8)
        return {'x': jax.random.normal(ks[0], (B, S, D_MODEL), dtype=jnp.float32), 'norm_w': jnp.ones((D_MODEL,), jnp.float32), 'norm_b': jnp.zeros((D_MODEL,), jnp.float32), 'W_in': jax.random.normal(ks[1], (D_INNER, D_MODEL), jnp.float32) * (1.0 / np.sqrt(D_MODEL)), 'b_in': jnp.zeros((D_INNER,), jnp.float32), 'A': jax.random.normal(ks[2], (D_INNER, D_STATE), jnp.float32), 'B_ssm': jax.random.normal(ks[3], (D_INNER, D_STATE), jnp.float32), 'C_ssm': jax.random.normal(ks[4], (D_INNER, D_STATE), jnp.float32), 'W_out': jax.random.normal(ks[5], (D_MODEL, D_INNER), jnp.float32) * (1.0 / np.sqrt(D_INNER)), 'b_out': jnp.zeros((D_MODEL,), jnp.float32)}
    _L0_attn_in = _L0_attn_setup()

    def _L0_ffn_setup():
        import jax, jax.numpy as jnp
        import numpy as np
        NHEAD = 16
        NUM_GROUPS = 4
        EXPERTS_PER_GROUP = 2
        LN_EPS = 1e-05

        def _layernorm(x, g, b):
            mu = jnp.mean(x, axis=-1, keepdims=True)
            var = jnp.mean(jnp.square(x - mu), axis=-1, keepdims=True)
            return (x - mu) * jax.lax.rsqrt(var + LN_EPS) * g + b

        def _mha(x, wi, bi, wo, bo):
            B, S, D = x.shape
            hd = D // NHEAD
            qkv = x @ wi.T + bi
            q, k, v = jnp.split(qkv, 3, axis=-1)

            def heads(t):
                return t.reshape(B, S, NHEAD, hd).transpose(0, 2, 1, 3)
            q, k, v = (heads(q), heads(k), heads(v))
            scores = jnp.einsum('bhqd,bhkd->bhqk', q, k) / jnp.sqrt(jnp.asarray(hd, x.dtype))
            attn = jax.nn.softmax(scores, axis=-1)
            o = jnp.einsum('bhqk,bhkd->bhqd', attn, v)
            o = o.transpose(0, 2, 1, 3).reshape(B, S, D)
            return o @ wo.T + bo

        def _hier_moe(x, w_group, b_group, w_expert, b_expert, w1, b1, w2, b2):
            B, S, D = x.shape
            xt = x.reshape(B * S, D)
            T = xt.shape[0]
            E = NUM_GROUPS * EXPERTS_PER_GROUP
            gp = jax.nn.softmax(xt @ w_group + b_group, axis=-1)
            g_idx = jnp.argmax(gp, axis=-1)
            g_prob = jnp.max(gp, axis=-1)
            elog = jnp.einsum('td,gde->tge', xt, w_expert) + b_expert
            ep = jax.nn.softmax(elog, axis=-1)
            ep_sel = jnp.take_along_axis(ep, g_idx[:, None, None], axis=1)[:, 0, :]
            e_idx_local = jnp.argmax(ep_sel, axis=-1)
            e_prob = jnp.max(ep_sel, axis=-1)
            flat_e = g_idx * EXPERTS_PER_GROUP + e_idx_local
            combine = jax.nn.one_hot(flat_e, E, dtype=xt.dtype) * (g_prob * e_prob)[:, None]
            h = jax.nn.relu(jnp.einsum('td,edf->etf', xt, w1) + b1[:, None, :])
            y = jnp.einsum('etf,efd->etd', h, w2) + b2[:, None, :]
            out = jnp.einsum('te,etd->td', combine, y)
            return out.reshape(B, S, D)
        key = jax.random.key(seed)
        ks = jax.random.split(key, 8)
        B, S, D, F = (2, 128, 128, 256)
        G, Epg = (NUM_GROUPS, EXPERTS_PER_GROUP)
        E = G * Epg
        sc = lambda fan: 1.0 / np.sqrt(fan)
        return {'x': jax.random.normal(ks[0], (B, S, D), jnp.float32), 'in_proj_w': jax.random.normal(ks[1], (3 * D, D), jnp.float32) * sc(D), 'in_proj_b': jnp.zeros((3 * D,), jnp.float32), 'out_proj_w': jax.random.normal(ks[2], (D, D), jnp.float32) * sc(D), 'out_proj_b': jnp.zeros((D,), jnp.float32), 'ln1_g': jnp.ones((D,), jnp.float32), 'ln1_b': jnp.zeros((D,), jnp.float32), 'ln2_g': jnp.ones((D,), jnp.float32), 'ln2_b': jnp.zeros((D,), jnp.float32), 'w_group': jax.random.normal(ks[3], (D, G), jnp.float32) * sc(D), 'b_group': jnp.zeros((G,), jnp.float32), 'w_expert': jax.random.normal(ks[4], (G, D, Epg), jnp.float32) * sc(D), 'b_expert': jnp.zeros((G, Epg), jnp.float32), 'w1': jax.random.normal(ks[5], (E, D, F), jnp.float32) * sc(D), 'b1': jnp.zeros((E, F), jnp.float32), 'w2': jax.random.normal(ks[6], (E, F, D), jnp.float32) * sc(F), 'b2': jnp.zeros((E, D), jnp.float32)}
    _L0_ffn_in = _L0_ffn_setup()

    def _L1_attn_setup():
        import jax, jax.numpy as jnp
        import numpy as np
        import math
        D_MODEL, D_C, D_R, NH = (128, 128, 32, 16)
        HD = D_MODEL // NH
        B, T = (2, 256)

        def _rope_tables(T, d_R):
            inv_freq = 1.0 / 10000.0 ** (jnp.arange(0, d_R, 2, dtype=jnp.float32) / d_R)
            t = jnp.arange(T, dtype=jnp.float32)
            freqs = jnp.outer(t, inv_freq)
            return (jnp.cos(freqs), jnp.sin(freqs))

        def _rotary_apply(x, cos, sin):
            d = x.shape[-1]
            x1, x2 = (x[..., :d // 2], x[..., d // 2:])
            return jnp.concatenate([x1 * cos - x2 * sin, x2 * cos + x1 * sin], axis=-1)
        key = jax.random.key(seed)
        ks = jax.random.split(key, 8)
        s = lambda fan_in: 1.0 / math.sqrt(fan_in)
        return {'x': jax.random.normal(ks[0], (B, T, D_MODEL), jnp.float32), 'W_kv_down': jax.random.normal(ks[1], (D_MODEL, D_C), jnp.float32) * s(D_MODEL), 'W_k_up': jax.random.normal(ks[2], (D_C, D_MODEL), jnp.float32) * s(D_C), 'W_v_up': jax.random.normal(ks[3], (D_C, D_MODEL), jnp.float32) * s(D_C), 'W_q': jax.random.normal(ks[4], (D_MODEL, D_MODEL), jnp.float32) * s(D_MODEL), 'W_q_rope': jax.random.normal(ks[5], (D_MODEL, D_R), jnp.float32) * s(D_MODEL), 'W_k_rope': jax.random.normal(ks[6], (D_C, D_R), jnp.float32) * s(D_C), 'W_o': jax.random.normal(ks[7], (D_MODEL, D_MODEL), jnp.float32) * s(D_MODEL)}
    _L1_attn_in = _L1_attn_setup()

    def _L1_ffn_setup():
        import jax, jax.numpy as jnp
        import numpy as np
        B, N, D, H, E = (4, 128, 128, 16, 8)
        DK = D // H
        HID = 4 * D
        EPS = 1e-05

        def _layernorm(x, w, b):
            m = jnp.mean(x, axis=-1, keepdims=True)
            v = jnp.mean(jnp.square(x - m), axis=-1, keepdims=True)
            return (x - m) * jax.lax.rsqrt(v + EPS) * w + b

        def _msa(x, w_qkv, w_proj):
            b, n, d = x.shape
            qkv = (x @ w_qkv).reshape(b, n, 3, H, DK)
            q = qkv[:, :, 0].transpose(0, 2, 1, 3)
            k = qkv[:, :, 1].transpose(0, 2, 1, 3)
            v = qkv[:, :, 2].transpose(0, 2, 1, 3)
            attn = jnp.einsum('bhnd,bhmd->bhnm', q, k) * (1.0 / np.sqrt(DK))
            attn = jax.nn.softmax(attn, axis=-1)
            y = jnp.einsum('bhnm,bhmd->bhnd', attn, v)
            y = y.transpose(0, 2, 1, 3).reshape(b, n, d)
            return y @ w_proj

        def _moe_mlp(x, gate_w, gate_b, w1, w2):
            b, n, d = x.shape
            xf = x.reshape(b * n, d)
            logits = xf @ gate_w + gate_b
            one_hot = jax.nn.one_hot(jnp.argmax(logits, axis=-1), E, dtype=xf.dtype)
            h = jax.nn.gelu(jnp.einsum('td,edh->teh', xf, w1), approximate=True)
            y = jnp.einsum('teh,ehd->ted', h, w2)
            out = jnp.einsum('te,ted->td', one_hot, y)
            return out.reshape(b, n, d)
        key = jax.random.key(seed)
        ks = jax.random.split(key, 8)
        s = 0.02
        return {'x': jax.random.normal(ks[0], (B, N, D), jnp.float32), 'ln1_w': jnp.ones((D,), jnp.float32), 'ln1_b': jnp.zeros((D,), jnp.float32), 'w_qkv': jax.random.normal(ks[1], (D, 3 * D), jnp.float32) * s, 'w_proj': jax.random.normal(ks[2], (D, D), jnp.float32) * s, 'ln2_w': jnp.ones((D,), jnp.float32), 'ln2_b': jnp.zeros((D,), jnp.float32), 'gate_w': jax.random.normal(ks[3], (D, E), jnp.float32) * s, 'gate_b': jnp.zeros((E,), jnp.float32), 'w1': jax.random.normal(ks[4], (E, D, HID), jnp.float32) * s, 'w2': jax.random.normal(ks[5], (E, HID, D), jnp.float32) * s}
    _L1_ffn_in = _L1_ffn_setup()
    _d = {'L0_attn_x': _L0_attn_in['x'], 'L0_attn_norm_w': _L0_attn_in['norm_w'], 'L0_attn_norm_b': _L0_attn_in['norm_b'], 'L0_attn_W_in': _L0_attn_in['W_in'], 'L0_attn_b_in': _L0_attn_in['b_in'], 'L0_attn_A': _L0_attn_in['A'], 'L0_attn_B_ssm': _L0_attn_in['B_ssm'], 'L0_attn_C_ssm': _L0_attn_in['C_ssm'], 'L0_attn_W_out': _L0_attn_in['W_out'], 'L0_attn_b_out': _L0_attn_in['b_out'], 'L0_ffn_in_proj_w': _L0_ffn_in['in_proj_w'], 'L0_ffn_in_proj_b': _L0_ffn_in['in_proj_b'], 'L0_ffn_out_proj_w': _L0_ffn_in['out_proj_w'], 'L0_ffn_out_proj_b': _L0_ffn_in['out_proj_b'], 'L0_ffn_ln1_g': _L0_ffn_in['ln1_g'], 'L0_ffn_ln1_b': _L0_ffn_in['ln1_b'], 'L0_ffn_ln2_g': _L0_ffn_in['ln2_g'], 'L0_ffn_ln2_b': _L0_ffn_in['ln2_b'], 'L0_ffn_w_group': _L0_ffn_in['w_group'], 'L0_ffn_b_group': _L0_ffn_in['b_group'], 'L0_ffn_w_expert': _L0_ffn_in['w_expert'], 'L0_ffn_b_expert': _L0_ffn_in['b_expert'], 'L0_ffn_w1': _L0_ffn_in['w1'], 'L0_ffn_b1': _L0_ffn_in['b1'], 'L0_ffn_w2': _L0_ffn_in['w2'], 'L0_ffn_b2': _L0_ffn_in['b2'], 'L1_attn_W_kv_down': _L1_attn_in['W_kv_down'], 'L1_attn_W_k_up': _L1_attn_in['W_k_up'], 'L1_attn_W_v_up': _L1_attn_in['W_v_up'], 'L1_attn_W_q': _L1_attn_in['W_q'], 'L1_attn_W_q_rope': _L1_attn_in['W_q_rope'], 'L1_attn_W_k_rope': _L1_attn_in['W_k_rope'], 'L1_attn_W_o': _L1_attn_in['W_o'], 'L1_ffn_ln1_w': _L1_ffn_in['ln1_w'], 'L1_ffn_ln1_b': _L1_ffn_in['ln1_b'], 'L1_ffn_w_qkv': _L1_ffn_in['w_qkv'], 'L1_ffn_w_proj': _L1_ffn_in['w_proj'], 'L1_ffn_ln2_w': _L1_ffn_in['ln2_w'], 'L1_ffn_ln2_b': _L1_ffn_in['ln2_b'], 'L1_ffn_gate_w': _L1_ffn_in['gate_w'], 'L1_ffn_gate_b': _L1_ffn_in['gate_b'], 'L1_ffn_w1': _L1_ffn_in['w1'], 'L1_ffn_w2': _L1_ffn_in['w2']}
    _x0 = _d['L0_attn_x']
    _d['L0_attn_x'] = jax.random.normal(jax.random.fold_in(jax.random.key(seed), 1), (4, 1024, 128), dtype=_x0.dtype)
    del _x0
    return _d

def reference(L0_attn_x, L0_attn_norm_w, L0_attn_norm_b, L0_attn_W_in, L0_attn_b_in, L0_attn_A, L0_attn_B_ssm, L0_attn_C_ssm, L0_attn_W_out, L0_attn_b_out, L0_ffn_in_proj_w, L0_ffn_in_proj_b, L0_ffn_out_proj_w, L0_ffn_out_proj_b, L0_ffn_ln1_g, L0_ffn_ln1_b, L0_ffn_ln2_g, L0_ffn_ln2_b, L0_ffn_w_group, L0_ffn_b_group, L0_ffn_w_expert, L0_ffn_b_expert, L0_ffn_w1, L0_ffn_b1, L0_ffn_w2, L0_ffn_b2, L1_attn_W_kv_down, L1_attn_W_k_up, L1_attn_W_v_up, L1_attn_W_q, L1_attn_W_q_rope, L1_attn_W_k_rope, L1_attn_W_o, L1_ffn_ln1_w, L1_ffn_ln1_b, L1_ffn_w_qkv, L1_ffn_w_proj, L1_ffn_ln2_w, L1_ffn_ln2_b, L1_ffn_gate_w, L1_ffn_gate_b, L1_ffn_w1, L1_ffn_w2):

    def _L0_attn_ref(x, norm_w, norm_b, W_in, b_in, A, B_ssm, C_ssm, W_out, b_out):
        import jax, jax.numpy as jnp
        import numpy as np
        D_MODEL, D_STATE, D_INNER = (128, 16, 256)
        B, S = (2, 512)
        EPS = 1e-05
        residual = x
        mu = jnp.mean(x, axis=-1, keepdims=True)
        var = jnp.mean(jnp.square(x - mu), axis=-1, keepdims=True)
        xn = (x - mu) * jax.lax.rsqrt(var + EPS) * norm_w + norm_b
        h = jnp.einsum('bsd,ed->bse', xn, W_in) + b_in
        a = jax.nn.sigmoid(jnp.einsum('bse,en->bsn', h, A))
        u = jnp.einsum('bse,en->bsn', h, B_ssm)

        def step(s, inp):
            a_t, u_t = inp
            s = s * a_t + u_t
            return (s, s)
        s0 = jnp.zeros((x.shape[0], D_STATE), x.dtype)
        _, states = jax.lax.scan(step, s0, (jnp.swapaxes(a, 0, 1), jnp.swapaxes(u, 0, 1)))
        y = jnp.einsum('sbn,en->bse', states, C_ssm)
        out = jnp.einsum('bse,de->bsd', y, W_out) + b_out
        return out + residual

    def _L0_ffn_ref(x, in_proj_w, in_proj_b, out_proj_w, out_proj_b, ln1_g, ln1_b, ln2_g, ln2_b, w_group, b_group, w_expert, b_expert, w1, b1, w2, b2):
        import jax, jax.numpy as jnp
        import numpy as np
        NHEAD = 16
        NUM_GROUPS = 4
        EXPERTS_PER_GROUP = 2
        LN_EPS = 1e-05

        def _layernorm(x, g, b):
            mu = jnp.mean(x, axis=-1, keepdims=True)
            var = jnp.mean(jnp.square(x - mu), axis=-1, keepdims=True)
            return (x - mu) * jax.lax.rsqrt(var + LN_EPS) * g + b

        def _mha(x, wi, bi, wo, bo):
            B, S, D = x.shape
            hd = D // NHEAD
            qkv = x @ wi.T + bi
            q, k, v = jnp.split(qkv, 3, axis=-1)

            def heads(t):
                return t.reshape(B, S, NHEAD, hd).transpose(0, 2, 1, 3)
            q, k, v = (heads(q), heads(k), heads(v))
            scores = jnp.einsum('bhqd,bhkd->bhqk', q, k) / jnp.sqrt(jnp.asarray(hd, x.dtype))
            attn = jax.nn.softmax(scores, axis=-1)
            o = jnp.einsum('bhqk,bhkd->bhqd', attn, v)
            o = o.transpose(0, 2, 1, 3).reshape(B, S, D)
            return o @ wo.T + bo

        def _hier_moe(x, w_group, b_group, w_expert, b_expert, w1, b1, w2, b2):
            B, S, D = x.shape
            xt = x.reshape(B * S, D)
            T = xt.shape[0]
            E = NUM_GROUPS * EXPERTS_PER_GROUP
            gp = jax.nn.softmax(xt @ w_group + b_group, axis=-1)
            g_idx = jnp.argmax(gp, axis=-1)
            g_prob = jnp.max(gp, axis=-1)
            elog = jnp.einsum('td,gde->tge', xt, w_expert) + b_expert
            ep = jax.nn.softmax(elog, axis=-1)
            ep_sel = jnp.take_along_axis(ep, g_idx[:, None, None], axis=1)[:, 0, :]
            e_idx_local = jnp.argmax(ep_sel, axis=-1)
            e_prob = jnp.max(ep_sel, axis=-1)
            flat_e = g_idx * EXPERTS_PER_GROUP + e_idx_local
            combine = jax.nn.one_hot(flat_e, E, dtype=xt.dtype) * (g_prob * e_prob)[:, None]
            h = jax.nn.relu(jnp.einsum('td,edf->etf', xt, w1) + b1[:, None, :])
            y = jnp.einsum('etf,efd->etd', h, w2) + b2[:, None, :]
            out = jnp.einsum('te,etd->td', combine, y)
            return out.reshape(B, S, D)
        attn_out = _mha(x, in_proj_w, in_proj_b, out_proj_w, out_proj_b)
        x = _layernorm(x + attn_out, ln1_g, ln1_b)
        moe_out = _hier_moe(x, w_group, b_group, w_expert, b_expert, w1, b1, w2, b2)
        x = _layernorm(x + moe_out, ln2_g, ln2_b)
        return x

    def _L1_attn_ref(x, W_kv_down, W_k_up, W_v_up, W_q, W_q_rope, W_k_rope, W_o):
        import jax, jax.numpy as jnp
        import numpy as np
        import math
        D_MODEL, D_C, D_R, NH = (128, 128, 32, 16)
        HD = D_MODEL // NH
        B, T = (2, 256)

        def _rope_tables(T, d_R):
            inv_freq = 1.0 / 10000.0 ** (jnp.arange(0, d_R, 2, dtype=jnp.float32) / d_R)
            t = jnp.arange(T, dtype=jnp.float32)
            freqs = jnp.outer(t, inv_freq)
            return (jnp.cos(freqs), jnp.sin(freqs))

        def _rotary_apply(x, cos, sin):
            d = x.shape[-1]
            x1, x2 = (x[..., :d // 2], x[..., d // 2:])
            return jnp.concatenate([x1 * cos - x2 * sin, x2 * cos + x1 * sin], axis=-1)
        Bb, Tt, _ = x.shape
        cos, sin = _rope_tables(Tt, D_R)
        cos = cos[None]
        sin = sin[None]
        c_kv = x @ W_kv_down
        k_rope = _rotary_apply(c_kv @ W_k_rope, cos, sin)
        k = (c_kv @ W_k_up).reshape(Bb, Tt, NH, HD)
        v = (c_kv @ W_v_up).reshape(Bb, Tt, NH, HD)
        q = (x @ W_q).reshape(Bb, Tt, NH, HD)
        q_rope = _rotary_apply(x @ W_q_rope, cos, sin)
        scale = math.sqrt(HD + D_R)
        scores = jnp.einsum('bqhd,bkhd->bhqk', q, k)
        scores = scores + jnp.einsum('bqr,bkr->bqk', q_rope, k_rope)[:, None]
        scores = scores / scale
        causal = jnp.triu(jnp.ones((Tt, Tt), dtype=bool), k=1)
        scores = jnp.where(causal[None, None], -jnp.inf, scores)
        w = jax.nn.softmax(scores, axis=-1)
        attn = jnp.einsum('bhqk,bkhd->bqhd', w, v).reshape(Bb, Tt, D_MODEL)
        return attn @ W_o

    def _L1_ffn_ref(x, ln1_w, ln1_b, w_qkv, w_proj, ln2_w, ln2_b, gate_w, gate_b, w1, w2):
        import jax, jax.numpy as jnp
        import numpy as np
        B, N, D, H, E = (4, 128, 128, 16, 8)
        DK = D // H
        HID = 4 * D
        EPS = 1e-05

        def _layernorm(x, w, b):
            m = jnp.mean(x, axis=-1, keepdims=True)
            v = jnp.mean(jnp.square(x - m), axis=-1, keepdims=True)
            return (x - m) * jax.lax.rsqrt(v + EPS) * w + b

        def _msa(x, w_qkv, w_proj):
            b, n, d = x.shape
            qkv = (x @ w_qkv).reshape(b, n, 3, H, DK)
            q = qkv[:, :, 0].transpose(0, 2, 1, 3)
            k = qkv[:, :, 1].transpose(0, 2, 1, 3)
            v = qkv[:, :, 2].transpose(0, 2, 1, 3)
            attn = jnp.einsum('bhnd,bhmd->bhnm', q, k) * (1.0 / np.sqrt(DK))
            attn = jax.nn.softmax(attn, axis=-1)
            y = jnp.einsum('bhnm,bhmd->bhnd', attn, v)
            y = y.transpose(0, 2, 1, 3).reshape(b, n, d)
            return y @ w_proj

        def _moe_mlp(x, gate_w, gate_b, w1, w2):
            b, n, d = x.shape
            xf = x.reshape(b * n, d)
            logits = xf @ gate_w + gate_b
            one_hot = jax.nn.one_hot(jnp.argmax(logits, axis=-1), E, dtype=xf.dtype)
            h = jax.nn.gelu(jnp.einsum('td,edh->teh', xf, w1), approximate=True)
            y = jnp.einsum('teh,ehd->ted', h, w2)
            out = jnp.einsum('te,ted->td', one_hot, y)
            return out.reshape(b, n, d)
        x = x + _msa(_layernorm(x, ln1_w, ln1_b), w_qkv, w_proj)
        x = x + _moe_mlp(_layernorm(x, ln2_w, ln2_b), gate_w, gate_b, w1, w2)
        return x
    x = L0_attn_x
    x = x + _L0_attn_ref(_layernorm(x, axis=-1), L0_attn_norm_w, L0_attn_norm_b, L0_attn_W_in, L0_attn_b_in, L0_attn_A, L0_attn_B_ssm, L0_attn_C_ssm, L0_attn_W_out, L0_attn_b_out)
    x = x + _L0_ffn_ref(_layernorm(x, axis=-1), L0_ffn_in_proj_w, L0_ffn_in_proj_b, L0_ffn_out_proj_w, L0_ffn_out_proj_b, L0_ffn_ln1_g, L0_ffn_ln1_b, L0_ffn_ln2_g, L0_ffn_ln2_b, L0_ffn_w_group, L0_ffn_b_group, L0_ffn_w_expert, L0_ffn_b_expert, L0_ffn_w1, L0_ffn_b1, L0_ffn_w2, L0_ffn_b2)
    x = x + _L1_attn_ref(_layernorm(x, axis=-1), L1_attn_W_kv_down, L1_attn_W_k_up, L1_attn_W_v_up, L1_attn_W_q, L1_attn_W_q_rope, L1_attn_W_k_rope, L1_attn_W_o)
    x = x + _L1_ffn_ref(_layernorm(x, axis=-1), L1_ffn_ln1_w, L1_ffn_ln1_b, L1_ffn_w_qkv, L1_ffn_w_proj, L1_ffn_ln2_w, L1_ffn_ln2_b, L1_ffn_gate_w, L1_ffn_gate_b, L1_ffn_w1, L1_ffn_w2)
    return x

_drawn_inputs = setup_inputs


def setup_inputs(seed=0):
    import zlib

    import numpy as np

    out = dict(_drawn_inputs(seed))
    spreads = {'L0_attn_norm_w': (1.0, 0.2),
     'L0_attn_norm_b': (0.0, 0.1),
     'L0_attn_b_in': (0.0, 0.1),
     'L0_attn_b_out': (0.0, 0.8),
     'L0_ffn_in_proj_b': (0.0, 0.8),
     'L0_ffn_out_proj_b': (0.0, 0.8),
     'L0_ffn_ln1_g': (1.0, 0.6),
     'L0_ffn_ln1_b': (0.0, 0.8),
     'L0_ffn_ln2_g': (1.0, 0.6),
     'L0_ffn_ln2_b': (0.0, 0.8),
     'L0_ffn_b_group': (0.0, 0.8),
     'L0_ffn_b_expert': (0.0, 2.0),
     'L0_ffn_b1': (0.0, 2.0),
     'L0_ffn_b2': (0.0, 2.0),
     'L1_ffn_ln1_w': (1.0, 0.6),
     'L1_ffn_ln1_b': (0.0, 2.0),
     'L1_ffn_ln2_w': (1.0, 0.6),
     'L1_ffn_ln2_b': (0.0, 2.0),
     'L1_ffn_gate_b': (0.0, 2.0)}
    factors = {'L0_ffn_in_proj_w': 8.0,
     'L0_ffn_out_proj_w': 8.0,
     'L0_ffn_w_group': 8.0,
     'L0_ffn_w_expert': 8.0,
     'L0_ffn_w1': 8.0,
     'L0_ffn_w2': 8.0,
     'L1_attn_W_kv_down': 8.0,
     'L1_attn_W_k_up': 8.0,
     'L1_attn_W_v_up': 8.0,
     'L1_attn_W_q': 8.0,
     'L1_attn_W_q_rope': 8.0,
     'L1_attn_W_k_rope': 8.0,
     'L1_attn_W_o': 8.0,
     'L1_ffn_w_qkv': 29.38,
     'L1_ffn_w_proj': 27.718,
     'L1_ffn_gate_w': 33.638,
     'L1_ffn_w1': 39.167,
     'L1_ffn_w2': 32.177}
    for name, (base, spread) in spreads.items():
        noise = np.random.default_rng([zlib.crc32(name.encode()), seed]).standard_normal(out[name].shape)
        drawn = base * np.exp(spread * noise) if base else spread * noise
        out[name] = jnp.asarray(drawn.astype(out[name].dtype))
    for name, factor in factors.items():
        out[name] = (out[name] * factor).astype(out[name].dtype)
    return out
```

```python
from contextlib import ExitStack

import numpy as np
import concourse.bass as bass
from concourse import mybir

F32 = mybir.dt.float32
BF16 = mybir.dt.bfloat16
ACT = mybir.ActivationFunctionType
ALU = mybir.AluOpType
AX = mybir.AxisListType

B, S, D = 4, 1024, 128
NT = 32
TB = 8
H, HD = 16, 8
UNITS = B * H
EPS = 1e-5
NEG = -1.0e30


class Tok:

    def __init__(self, eng):
        self.eng, self.need, self.sem, self.val = eng, False, None, 0


class Queues:

    ENG = ("tensor", "scalar", "vector", "gpsimd", "sync")

    def __init__(self, nc, ctx):
        self.nc, self.ctx = nc, ctx
        self.q = {e: [] for e in self.ENG}
        self.last = {e: None for e in self.ENG}
        self.dma_n = {}
        self.dma_sems = {}
        self.dma_open = []

    def op(self, eng, fn, *waits):
        t = Tok(eng)
        self.q[eng].append((self.flat(waits), fn, t))
        self.last[eng] = t
        return t

    def pe(self, fn, *w):
        return self.op("tensor", fn, *w)

    def act(self, fn, *w):
        return self.op("scalar", fn, *w)

    def dve(self, fn, *w):
        return self.op("vector", fn, *w)

    def pool(self, fn, *w):
        return self.op("gpsimd", fn, *w)

    def flat(self, waits):
        out = []
        for w in waits:
            if isinstance(w, Tok):
                w.need = True
                out.append(w)
            elif w:
                out.extend(self.flat(w))
        return out

    def dma(self, stream, dst, src, *waits, eng="sync"):
        n = self.dma_n.get(stream, 0)
        self.dma_n[stream] = n + 1
        if stream not in self.dma_sems:
            self.dma_sems[stream] = self.ctx.enter_context(self.nc.semaphore("d_" + stream))
        t = Tok("dma")
        t.need, t.sem, t.val = True, self.dma_sems[stream], 16 * (n + 1)
        self.q[eng].append((self.flat(waits), lambda e: e.dma_start(dst, src), t))
        self.dma_open.append(t)
        return t

    def barrier(self, *extra):
        ends = [self.last[e] for e in ("tensor", "scalar", "vector", "gpsimd") if self.last[e] is not None]
        for e in self.ENG:
            self.q[e].append((self.flat([ends, extra]), None, None))
        return ends

    def finish(self, toks):
        self.q["sync"].append((self.flat([toks]), None, None))

    def emit(self, block):
        for e in ("tensor", "scalar", "vector", "gpsimd"):
            sem = self.ctx.enter_context(self.nc.semaphore("s_" + e))
            n = 0
            for _, _, t in self.q[e]:
                if t is not None and t.eng == e and t.need:
                    n += 1
                    t.sem, t.val = sem, n

        def program(name):
            def run(eng):
                seen = {}
                for waits, fn, t in self.q[name]:
                    best = {}
                    for w in waits:
                        if w.val > best.get(id(w.sem), (None, 0))[1]:
                            best[id(w.sem)] = (w.sem, w.val)
                    for k, (s, v) in best.items():
                        if seen.get(k, 0) < v:
                            eng.wait_ge(s, v)
                            seen[k] = v
                    if fn is None:
                        continue
                    ins = fn(eng)
                    if t.eng == "dma":
                        ins.then_inc(t.sem, 16)
                    elif t.need:
                        ins.then_inc(t.sem, 1)
            return run

        block.tensor(program("tensor"))
        block.scalar(program("scalar"))
        block.vector(program("vector"))
        block.gpsimd(program("gpsimd"))
        block.sync(program("sync"))


class Bank:

    def __init__(self, t):
        self.t, self.free = t, None


def build(nc, ins, out):
    with ExitStack() as ctx:
        q = Queues(nc, ctx)

        def sb(name, shape, dt=F32):
            return ctx.enter_context(nc.sbuf_tensor(name, shape, dt))

        X = sb("X", [128, NT, 128])
        Z = sb("Z", [128, NT, 128])
        W = sb("W", [128, NT, 128])
        ZT = sb("ZT", [128, NT * 128])
        VP = sb("VP", [128, NT, 168])
        PB = sb("PB", [128, 12, 512])
        NB = 4
        RK = sb("RK", [128, NB, 4, 1024], BF16)
        W1 = sb("W1", [128, 8 * 512])
        W2 = sb("W2", [128, 8 * 4 * 128])
        OS = sb("OS", [128, 2, 512])
        WT = sb("WT", [128, 1920])
        identf = sb("identf", [128, 128])
        identb = sb("identb", [128, 128], BF16)
        maskb = sb("maskb", [128, 384], BF16)
        sel = sb("sel", [128, 18])
        bc = sb("bc", [128, 6, 128])
        cols = sb("cols", [128, 40])
        st = sb("st", [128, NT, 6])
        mv = sb("mv", [128, NT, 2])
        rs = sb("rs", [128, 4, NT])
        small = sb("small", [128, 4, 64])
        nms = sb("nms", [24, 4, 128], BF16)
        gs = sb("gs", [128, 14, NT * 8])
        ctt = OS[0:8, :, :]
        b2s = sb("b2s", [8, 128])
        bank = [Bank(ctx.enter_context(nc.psum_tensor(f"bank{i}", [128, 512], F32))) for i in range(8)]
        QD = nc.dram_tensor("q_parts", (B, 5, 128, 1024), BF16, kind="Internal").ap()
        KD = nc.dram_tensor("k_parts", (B, 5, 128, 1024), BF16, kind="Internal").ap()
        RD = nc.dram_tensor("r_parts", (B, 3, 64, 1024), BF16, kind="Internal").ap()

        def load(stream, dst, src, *w, eng="sync"):
            return q.dma(stream, dst, src, *w, eng=eng)

        xin = ins["x"].rearrange("(t p) d -> p t d", p=128)
        tx = [q.dma("x%d" % b, X[:, 8 * b:8 * b + 8, :], xin[:, 8 * b:8 * b + 8, :]) for b in range(B)]
        t_cols = load("c_cols", cols[:, :], ins["cols"], eng="scalar")
        t_idf = load("c_idf", identf[:, :], ins["identf"], eng="scalar")
        t_idb = load("c_idb", identb[:, :], ins["identb"], eng="scalar")
        t_mask = load("c_mask", maskb[:, :], ins["maskb"], eng="scalar")
        t_sel = load("c_sel", sel[:, :], ins["sel"], eng="scalar")
        t_bc = load("c_bc", bc[:, :, :], ins["rows"].partition_broadcast(128), eng="scalar")
        wssm = WT[:, 0:1280]
        t_ws = load("c_ws", wssm, ins["w_ssm"], eng="scalar")

        def ln_stats(src, b, *w):
            lo, hi = 8 * b, 8 * b + 8
            a = [q.dve(lambda e, t=t: e.bn_stats(st[:, t, :], src[:, t, :]), *w) for t in range(lo, hi)]
            g = [q.dve(lambda e, t=t: e.bn_aggr(mv[:, t, :], st[:, t, :]), a[t - lo]) for t in range(lo, hi)]
            ve, sd, r, n = (rs[:, i, lo:hi] for i in range(4))
            t1 = q.dve(lambda e: e.tensor_scalar(ve, mv[:, lo:hi, 1], EPS, None, ALU.add), g[-1])
            t2 = q.act(lambda e: e.activation(sd, ve, ACT.Sqrt), t1)
            t3 = q.dve(lambda e: e.reciprocal(r, sd), t2)
            t4 = q.dve(lambda e: e.tensor_tensor(n, r, r, ALU.mult), t3)
            t5 = q.dve(lambda e: e.tensor_tensor(n, n, ve, ALU.mult), t4)
            t6 = q.dve(lambda e: e.tensor_scalar(n, n, -0.5, 1.5, ALU.mult, ALU.add), t5)
            return q.dve(lambda e: e.tensor_tensor(r, r, n, ALU.mult), t6)

        def ln_apply(dst, src, b, t_r):
            for t in range(8 * b, 8 * b + 8):
                k = q.dve(lambda e, t=t: e.tensor_scalar(dst[:, t, :], src[:, t, :], mv[:, t, 0:1], rs[:, 2, t:t + 1],
                                                         ALU.subtract, ALU.mult), t_r)
            return k

        def transposed(src, b, t_src, dst, scale=None, bias=None, pair=(6, 7)):
            toks = []
            for c in range(2 * b, 2 * b + 2):
                bk = bank[pair[c % 2]]
                for j in range(4):
                    p = q.pe(lambda e, j=j, c=c, bk=bk: e.transpose(bk.t[:, 128 * j:128 * j + 128], src[:, 4 * c + j, :],
                                                                    identf[:, :]), t_src, bk.free, t_idf)
                o = dst[:, 512 * c:512 * c + 512]
                if scale is None:
                    bk.free = q.act(lambda e, o=o, bk=bk: e.activation(o, bk.t[:, :], ACT.Copy), p)
                else:
                    bk.free = q.act(lambda e, o=o, bk=bk: e.activation(o, bk.t[:, :], ACT.Identity, bias=bias,
                                                                       scale=scale), p, t_cols)
                toks.append(bk.free)
            return toks

        t_ssm_in = []
        t_z0 = []
        for b in range(B):
            r = ln_stats(X, b, tx[b])
            z = ln_apply(Z, X, b, r)
            t_z0.append(z)
            r2 = ln_stats(Z, b, z)
            z2 = ln_apply(W, Z, b, r2)
            t_ssm_in += transposed(W, b, z2, ZT, scale=cols[:, 0:1], bias=cols[:, 1:2])
        w_in = wssm[:, 0:256].rearrange("p (c n) -> p c n", c=2)
        a_rep = wssm[:, 256:512].rearrange("p (c n) -> p c n", c=2)
        b_rep = wssm[:, 512:768].rearrange("p (c n) -> p c n", c=2)
        c_rep = wssm[:, 768:1024].rearrange("p (c n) -> p c n", c=2)
        wo_t = wssm[:, 1024:1280].rearrange("p (c n) -> p c n", c=2)
        gsb = WT[:, 1280:1344]
        h4 = WT[:, 1344:1472]
        bb = cols[:, 36:40]
        bk = bank[0]
        for c in range(2):
            q.pe(lambda e, c=c: e.matmul(bk.t[:, 0:32], w_in[:, c, :], a_rep[:, c, 0:32], start=(c == 0), stop=(c == 1)), t_ws)
        for c in range(2):
            p = q.pe(lambda e, c=c: e.matmul(bk.t[:, 32:64], w_in[:, c, :], b_rep[:, c, 0:32], start=(c == 0), stop=(c == 1)))
        t_g = q.act(lambda e: e.activation(gsb, bk.t[:, 0:64], ACT.Copy), p)
        bk1 = bank[1]
        for c in range(2):
            p = q.pe(lambda e, c=c: e.matmul(bk1.t[:, 0:128], c_rep[:, c, :], wo_t[:, c, :], start=(c == 0), stop=(c == 1)))
        t_h = q.act(lambda e: e.activation(h4, bk1.t[:, 0:128], ACT.Copy), p)
        bk2 = bank[2]
        for i, rep in enumerate((a_rep, b_rep)):
            for c in range(2):
                p = q.pe(lambda e, c=c, i=i, rep=rep: e.matmul(bk2.t[:, i:i + 1], rep[:, c, :], cols[:, 2 + c:3 + c],
                                                               start=(c == 0), stop=(c == 1)), t_cols)
        t_b1 = q.dve(lambda e: e.tensor_scalar(bb[:, 0:1], bk2.t[:, 0:1], -1.0, None, ALU.mult), p)
        t_b2 = q.dve(lambda e: e.tensor_copy(bb[:, 1:2], bk2.t[:, 1:2]), p)
        q.barrier()
        A_s, U_s, S_s = PB[:, 0:2, :], PB[:, 2:4, :], PB[:, 4:6, :]
        pa = []
        for i, base in ((0, 2), (1, 4)):
            for hf in range(2):
                for b in range(B):
                    p = q.pe(lambda e, i=i, base=base, hf=hf, b=b: e.matmul(
                        bank[base + hf].t[32 * b:32 * b + 32, :], gsb[:, 32 * i:32 * i + 32],
                        ZT[:, 1024 * b + 512 * hf:1024 * b + 512 * hf + 512], start=True, stop=True), t_g)
                pa.append(p)
        ta = []
        for hf in range(2):
            x = q.act(lambda e, hf=hf: e.activation(A_s[:, hf, :], bank[2 + hf].t[:, :], ACT.Exp, bias=bb[:, 0:1],
                                                    scale=-1.0), pa[hf], t_b1)
            y = q.dve(lambda e, hf=hf: e.tensor_scalar(A_s[:, hf, :], A_s[:, hf, :], 1.0, None, ALU.add), x)
            ta.append(q.dve(lambda e, hf=hf: e.reciprocal(A_s[:, hf, :], A_s[:, hf, :]), y))
            tu = q.act(lambda e, hf=hf: e.activation(U_s[:, hf, :], bank[4 + hf].t[:, :], ACT.Identity, bias=bb[:, 1:2]),
                       pa[2 + hf], t_b2)
            ta.append(tu)
        t_scan = q.dve(lambda e: e.tensor_tensor_scan(S_s.rearrange("p a b -> p (a b)"), A_s.rearrange("p a b -> p (a b)"),
                                                      U_s.rearrange("p a b -> p (a b)"), 0.0, ALU.mult, ALU.add), ta)
        t_x = []
        for b in range(B):
            zs = Z[:, 8 * b:8 * b + 8, :]
            p1 = q.pool(lambda e, zs=zs: e.tensor_tensor(zs, zs, bc[:, 0:1, :].broadcast_to((128, 8, 128)), ALU.add), t_bc)
            xs = X[:, 8 * b:8 * b + 8, :]
            t_x.append(q.pool(lambda e, xs=xs, zs=zs: e.tensor_tensor(xs, xs, zs, ALU.add), p1))
        sv = S_s.rearrange("p a b -> p (a b)")
        for c in range(8):
            b = c // 2
            bk = bank[c % 2]
            for j in range(4):
                tt = (4 * c + j) % 8
                p = q.pe(lambda e, b=b, bk=bk, j=j, tt=tt: e.matmul(
                    bk.t[:, 128 * j:128 * j + 128], sv[32 * b:32 * b + 32, 128 * tt:128 * tt + 128],
                    h4[32 * b:32 * b + 32, :], start=True, stop=True), t_scan, t_h, bk.free if c > 1 else None)
            xs = X[:, 4 * c:4 * c + 4, :].rearrange("p a b -> p (a b)")
            bk.free = q.dve(lambda e, xs=xs, bk=bk: e.tensor_tensor(xs, xs, bk.t[:, :], ALU.add), p, t_x[b])
            t_x[b] = bk.free
        q.barrier()

        t_vz = q.pool(lambda e: e.memset(VP[:, :, 144:168], 0.0))
        VH = VP[:, :, 0:144].rearrange("p t (h c) -> p t h c", c=9)
        t_vo = q.pool(lambda e: e.memset(VH[:, :, :, 8:9], 1.0))

        def attention(layer, wq, wk, wv, qb, kb, vb, wrope, t_w, t_zt):
            causal = layer == 1
            scale = 1.0 / float(np.sqrt(40.0 if causal else 8.0))
            for bkk in bank:
                bkk.free = None
            wr = {}
            tmp = PB
            nslot = [0]

            def parts(pt, rows, bias, dst, five, c, extra=None):
                s = nslot[0] % 3
                n = nslot[0]
                nslot[0] += 1
                prev = slot_done[s]
                x = tmp[0:rows, 3 * s, :]
                r1 = tmp[0:rows, 3 * s + 1, :]
                sp = tmp[0:rows, 3 * s + 2, :].bitcast(BF16)
                sp3 = lo3[0:rows, s, :]
                hi, mid, lo = sp[:, 0:512], sp[:, 512:1024], sp3
                bkk, p = pt
                if extra is None:
                    x1 = q.act(lambda e: e.activation(x, bkk.t[0:rows, :], ACT.Identity, bias=bias), p, prev, t_cols)
                    bkk.free = x1
                else:
                    x1 = extra(x, prev)
                h1 = q.dve(lambda e: e.tensor_copy(hi, x), x1, prev)
                d1 = q.dve(lambda e: e.tensor_tensor(r1, x, hi, ALU.subtract), h1)
                d2 = q.dve(lambda e: e.tensor_copy(mid, r1), d1)
                d3 = q.dve(lambda e: e.tensor_tensor(lo, r1, mid, ALU.subtract), d2)
                b, tc = c // 2, slice(512 * (c % 2), 512 * (c % 2) + 512)
                ds = []
                for k, src in enumerate((hi, mid, lo)):
                    tgt = (k, k + 3) if five and k < 2 else (k,)
                    for m in tgt:
                        ds.append(q.dma("sc%d" % s, dst[b, m, 0:rows, tc], src, d3))
                slot_done[s] = ds
                wr.setdefault(b, []).extend(ds)

            slot_done = [None] * 3
            lo3 = OS[:, :, :].rearrange("p a b -> p (a b)").bitcast(BF16)[:, 0:1536].rearrange("p (s n) -> p s n", s=3)
            kk = 0
            for c in range(8):
                for wt, bias, dst in ((wq, qb, QD), (wk, kb, KD)):
                    bkk = bank[kk % 4]
                    kk += 1
                    p = q.pe(lambda e, bkk=bkk, wt=wt, c=c: e.matmul(bkk.t[:, :], wt, ZT[:, 512 * c:512 * c + 512],
                                                                     start=True, stop=True), bkk.free, t_w, t_zt)
                    parts((bkk, p), 128, bias, dst, True, c)
                if causal:
                    b0, b1 = bank[4], bank[5]
                    p0 = q.pe(lambda e, c=c: e.matmul(b0.t[0:64, :], wrope[0], ZT[:, 512 * c:512 * c + 512], start=True,
                                                      stop=True), b0.free)
                    p1 = q.pe(lambda e, c=c: e.matmul(b1.t[0:64, :], wrope[1], ZT[:, 512 * c:512 * c + 512], start=True,
                                                      stop=True), b1.free)

                    def rot(x, prev, c=c, p0=p0, p1=p1):
                        o = 512 * (c % 2)
                        m0 = q.dve(lambda e: e.tensor_tensor(x, b0.t[0:64, :], W1[0:64, o:o + 512], ALU.mult), p0, prev, t_w)
                        y = OS2[0:64, :]
                        m1 = q.dve(lambda e: e.tensor_tensor(y, b1.t[0:64, :], W1[0:64, 1024 + o:1536 + o], ALU.mult), p1)
                        b0.free, b1.free = m0, m1
                        return q.dve(lambda e: e.tensor_tensor(x, x, y, ALU.add), m1)
                    parts((b0, p0), 64, None, RD, False, c, rot)
                bkk = bank[6 + c % 2]
                for j in range(4):
                    p = q.pe(lambda e, bkk=bkk, c=c, j=j: e.matmul(bkk.t[:, 128 * j:128 * j + 128],
                                                                   ZT[:, 512 * c + 128 * j:512 * c + 128 * j + 128], wv,
                                                                   start=True, stop=True), bkk.free)
                o = VH[:, 4 * c:4 * c + 4, :, 0:8]
                i0 = bkk.t[:, :].rearrange("p (t h c) -> p t h c", t=4, c=8)
                for j in range(4):
                    if vb is None:
                        bkk.free = q.act(lambda e, o=o, i0=i0, j=j: e.activation(o[:, j], i0[:, j], ACT.Copy), p)
                    else:
                        bkk.free = q.dve(lambda e, o=o, i0=i0, j=j: e.tensor_tensor(
                            o[:, j], i0[:, j], vb.rearrange("p (h c) -> p h c", c=8), ALU.add), p, t_bc)
            t_v = bkk.free
            q.barrier(slot_done)

            if causal:
                KR, Z0, M0 = 128, 24, 24
            else:
                KR, Z0, M0 = 96, 72, 72
            t_fill = []
            for s in range(NB):
                z0, z1 = (0, 32) if causal else (64, 96)
                t_fill.append(q.pool(lambda e, s=s, z0=z0, z1=z1: e.memset(RK[z0:z1, s, :, :], 0.0)))
            ones_t = [q.dma("ld%d" % s, RK[M0:M0 + 3, s, 1, :], ins["ones"], t_fill[s]) for s in range(NB)]
            loaded = {}
            mained = {}
            maxed = {}

            def fetch(u):
                s, b, h = u % NB, u // H, u % H
                r = slice(8 * h, 8 * h + 8)
                w = [t_fill[s], ones_t[s], wr[b], mained.get(u - NB)]
                L = []

                def cp(k, row, src, n):
                    dst = RK[row:row + 8 * n, s, k, :]
                    L.append(q.dma("ld%d" % s, dst, src, w))
                if causal:
                    cp(0, 0, QD[b, 0:2, r, :], 2)
                    cp(0, 16, QD[b, 0:1, r, :], 1)
                    cp(1, 0, KD[b, 0:1, r, :], 1)
                    cp(1, 8, KD[b, 0:2, r, :], 2)
                    cp(2, 0, QD[b, 0:3, r, :], 3)
                    for i in range(3):
                        cp(3, 8 * i, KD[b, 2 - i:3 - i, r, :], 1)
                    if h < NB:
                        for k, off, ps in ((0, 0, (0, 1, 0)), (1, 32, (0, 0, 1)), (2, 0, (0, 1, 2)), (3, 32, (2, 1, 0))):
                            for i in range(3):
                                L.append(q.dma("ld%d" % s, RK[32 + 32 * i:64 + 32 * i, s, k, :],
                                               RD[b, ps[i], off:off + 32, :], w))
                else:
                    for i in range(3):
                        cp(0, 24 * i, QD[b, i:i + 3, r, :], 3)
                        cp(1, 24 * i, KD[b, 0:3, r, :], 3)
                if u >= NB:
                    L.append(q.dma("ld%d" % s, RK[M0:M0 + 3, s, 0, :], ins["zeros"], w))
                loaded[u] = L

            if causal:
                mains = [(kt, qh, max(0, 128 * kt - 512 * qh) if kt != 1 else 0) for kt in range(8)
                         for qh in range(kt // 4, 2)]
                maxes = [(qt, kh, min(512, 128 * (qt + 1) - 512 * kh)) for qt in range(8) for kh in range(qt // 4 + 1)]
                t_m2 = q.pool(lambda e: e.memset(small[:, 0:2, 0:16], NEG))
            else:
                mains = [(kt, qh, 0) for kt in range(8) for qh in range(2)]
                maxes = [(qt, kh, 512) for qt in range(8) for kh in range(2)]
                t_m2 = None
            n = len(mains)
            assert len(maxes) == n
            bmain, bmax, bav, bsel, btr = bank[0:3], bank[3:5], bank[5], bank[6], bank[7]
            t_nm = {}
            mcount = [0]
            xcount = [0]

            def max_step(u, i):
                s = u % NB
                qt, kh, wd = maxes[i]
                bkk = bmax[xcount[0] % 2]
                xcount[0] += 1
                diag = causal and kh == qt // 4
                ks = slice(512 * kh, 512 * kh + wd)
                w = loaded[u] if i == 0 else None
                p = q.pe(lambda e: e.matmul(bkk.t[:, 0:wd], RK[0:KR, s, 0, 128 * qt:128 * qt + 128], RK[0:KR, s, 1, ks],
                                            start=True, stop=not diag), bkk.free, w)
                if diag:
                    p = q.pe(lambda e: e.matmul(bkk.t[:, wd - 128:wd], identb[:, :], maskb[:, 0:128], start=False,
                                                stop=True), t_idb, t_mask)
                m2 = small[:, u % 2, 0:16]
                bkk.free = q.dve(lambda e: e.tensor_reduce(m2[:, 2 * qt + kh:2 * qt + kh + 1], bkk.t[:, 0:wd], AX.X,
                                                           ALU.max), p, t_m2)
                if i == n - 1:
                    maxed[u] = bkk.free

            def max_end(u):
                s, k = u % NB, u % 2
                m2 = small[:, k, 0:16]
                nm = small[:, k, 16:24]
                r1 = small[:, k, 24:32]
                pts = small[:, 2 + k, 0:32].bitcast(BF16)
                a = q.dve(lambda e: e.tensor_reduce(nm, m2.rearrange("p (a b) -> p a b", b=2), AX.X, ALU.max, negate=True),
                          maxed[u])
                b_ = q.dve(lambda e: e.tensor_copy(pts[:, 0:8], nm), a)
                c = q.dve(lambda e: e.tensor_tensor(r1, nm, pts[:, 0:8], ALU.subtract), b_)
                d = q.dve(lambda e: e.tensor_copy(pts[:, 8:16], r1), c)
                f = q.dve(lambda e: e.tensor_tensor(pts[:, 16:24], r1, pts[:, 8:16], ALU.subtract), d)
                t_nm[u] = f

            def max_send(u):
                s, k = u % NB, u % 2
                pts = small[:, 2 + k, 0:32].bitcast(BF16)
                tb = btr.t[0:24, 0:64].bitcast(BF16)
                p = q.pe(lambda e: e.transpose(tb, pts[:, 0:24], identb[:, :]), t_nm[u], btr.free, t_idb)
                o = nms[:, u % 4, :]
                btr.free = q.dve(lambda e: e.tensor_copy(o, tb), p, sent.get(u - 4))
                sent[u] = [q.dma("nm%d" % (u % 4), RK[M0 + i:M0 + i + 1, s, 0, :], nms[8 * i:8 * i + 8, u % 4, :], btr.free,
                                 loaded[u], maxed[u]) for i in range(3)]

            sent = {}
            t_exp = {}
            t_av = {}
            NPB = 12

            def main_step(u, i):
                s = u % NB
                kt, qh, c0 = mains[i]
                g = u * n + i
                bkk = bmain[g % 3]
                w = sent[u] if i == 0 else None
                qs = slice(512 * qh + c0, 512 * qh + 512)
                diag = causal and (kt // 4 == qh)
                p = q.pe(lambda e: e.matmul(bkk.t[:, c0:512], RK[0:KR, s, 1, 128 * kt:128 * kt + 128], RK[0:KR, s, 0, qs],
                                            start=True, stop=not causal), bkk.free, w)
                if causal:
                    p = q.pe(lambda e: e.matmul(bkk.t[:, c0:512], RK[0:KR, s, 3, 128 * kt:128 * kt + 128],
                                                RK[0:KR, s, 2, qs], start=False, stop=not diag))
                if diag:
                    if kt == 1:
                        p = q.pe(lambda e: e.matmul(bkk.t[:, 0:256], identb[:, :], maskb[:, 128:384], start=False,
                                                    stop=True))
                    else:
                        p = q.pe(lambda e: e.matmul(bkk.t[:, c0:c0 + 128], identb[:, :], maskb[:, 256:384], start=False,
                                                    stop=True))
                if i == n - 1:
                    mained[u] = p
                o = PB[:, g % NPB, c0:512]
                bkk.free = q.act(lambda e: e.activation(o, bkk.t[:, c0:512], ACT.Exp, scale=scale), p,
                                 t_av.get(g - NPB))
                t_exp[g] = bkk.free

            starts = [min(i for i, m in enumerate(mains) if (m[0] % 2, m[1]) == k) for k in ((0, 0), (0, 1), (1, 0), (1, 1))]
            ends = [max(i for i, m in enumerate(mains) if (m[0] % 2, m[1]) == k) for k in ((0, 0), (0, 1), (1, 0), (1, 1))]

            def av_group(gg):
                for g in range(4 * gg, 4 * gg + 4):
                    u, i = g // n, g % n
                    b, h = u // H, u % H
                    kt, qh, c0 = mains[i]
                    j = 2 * (kt % 2) + qh
                    p = q.pe(lambda e, g=g, i=i, b=b, h=h, kt=kt, c0=c0, j=j: e.matmul(
                        bav.t[32 * j:32 * j + 32, c0:512], VP[:, 8 * b + kt, 9 * h:9 * h + 32], PB[:, g % NPB, c0:512],
                        start=(i in starts), stop=(i in ends)), t_exp[g], bav.free, t_v, t_vz, t_vo)
                    t_av[g] = p
                return p

            def out_copy(u, p):
                o = OS[:, u % 2, :]
                bav.free = q.act(lambda e: e.activation(o, bav.t[:, :], ACT.Copy), p, t_os.get(u - 2))
                return bav.free

            t_os = {}
            done_w = {}

            def out_norm(u, t_o):
                b, h = u // H, u % H
                for c in range(4):
                    p = q.pe(lambda e, c=c: e.matmul(bsel.t[:, 18 * c:18 * c + 18], OS[:, u % 2, 128 * c:128 * c + 128],
                                                     sel[:, :], start=True, stop=True), t_o, bsel.free, t_sel)
                t_os[u] = p
                v = bsel.t[:, 0:72].rearrange("p (c f k) -> p c f k", c=4, k=9)
                rc = small[:, u % 2, 32:40].rearrange("p (c f) -> p c f", f=2)
                r = q.dve(lambda e: e.reciprocal(rc, v[:, :, :, 8]), p)
                for f in range(2):
                    wv_ = W[:, 8 * b + 4 * f:8 * b + 4 * f + 4, 8 * h:8 * h + 8]
                    bsel.free = q.dve(lambda e, f=f, wv_=wv_: e.tensor_tensor(
                        wv_, v[:, :, f, 0:8], rc[:, :, f:f + 1].broadcast_to((128, 4, 8)), ALU.mult), r)
                done_w[b] = bsel.free

            LA = 2
            for u in range(3):
                fetch(u)
            pend_o = None
            for u in range(-LA, UNITS + 1):
                for i in range(n):
                    um = u + LA
                    if um < UNITS:
                        max_step(um, i)
                    if 0 <= u < UNITS:
                        main_step(u, i)
                        g = u * n + i
                        if g % 4 == 3 and g >= 7:
                            p = av_group(g // 4 - 1)
                            if (g // 4) % (n // 4) == 0:
                                pend_o = (u - 1, out_copy(u - 1, p))
                    elif u == UNITS and i == 3:
                        p = av_group(UNITS * n // 4 - 1)
                        pend_o = (u - 1, out_copy(u - 1, p))
                    if i == 7 and pend_o is not None:
                        out_norm(*pend_o)
                        pend_o = None
                    if i == 1 and 0 <= um - 1 < UNITS:
                        max_end(um - 1)
                    if i == 4 and 0 <= um - 1 < UNITS:
                        max_send(um - 1)
                nx = u + LA + 1
                if 3 <= nx < UNITS:
                    fetch(nx)
            q.barrier()
            for bkk in bank:
                bkk.free = None

        def project(wo, t_w, resid, dst, bias_row):
            toks = []
            for b in range(B):
                t = transposed(W, b, None, ZT)
                for c in (2 * b, 2 * b + 1):
                    bk = bank[c % 2]
                    for j in range(4):
                        k = 4 * c + j
                        p = q.pe(lambda e, bk=bk, j=j, k=k: e.matmul(bk.t[:, 128 * j:128 * j + 128],
                                                                     ZT[:, 128 * k:128 * k + 128], wo, start=True,
                                                                     stop=True), t, bk.free, t_w)
                    o = dst[:, 4 * c:4 * c + 4, :]
                    r = resid[:, 4 * c:4 * c + 4, :]
                    v = bk.t[:, :].rearrange("p (a b) -> p a b", a=4)
                    bk.free = q.dve(lambda e, o=o, r=r, v=v: e.tensor_tensor(o, r, v, ALU.add), p)
                    last = bk.free
                    if bias_row is not None:
                        last = q.dve(lambda e, o=o: e.tensor_tensor(o, o, bc[:, bias_row:bias_row + 1, :].broadcast_to(
                            (128, 4, 128)), ALU.add), bk.free, t_bc)
                toks.append(last)
            return toks

        def moe(nf, func, t_w, t_c, t_zt, t_ct, has_bias):
            cc = gs[:, 0, :].rearrange("p (t k) -> p t k", k=8)
            bh, by = bank[0:4], bank[4:6]
            hc = 0
            yc = 0
            t_y = {}
            hs = {}
            accs = {}

            def down(c, e, ht):
                nonlocal yc
                bk = by[yc % 2]
                yc += 1
                for j in range(4):
                    for f in range(nf):
                        k = (e % 2) * nf + f
                        p = q.pe(lambda en, bk=bk, j=j, f=f, k=k, e=e: en.matmul(
                            bk.t[:, 128 * j:128 * j + 128], PB[:, k, 128 * j:128 * j + 128],
                            W2[:, 128 * (e * nf + f):128 * (e * nf + f) + 128], start=(f == 0), stop=(f == nf - 1)),
                            ht, bk.free)
                t_y[(c, e)] = p
                for j in range(4):
                    t = 4 * c + j
                    o, v = W[:, t, :], bk.t[:, 128 * j:128 * j + 128]
                    s = cc[:, t, e:e + 1]
                    if (c, j) not in accs:
                        bk.free = q.dve(lambda en, o=o, v=v, s=s: en.tensor_scalar(o, v, s, None, ALU.mult), p, t_c)
                    else:
                        bk.free = q.dve(lambda en, o=o, v=v, s=s: en.scalar_tensor_tensor(
                            out=o, in0=v, scalar=s, in1=o, op0=ALU.mult, op1=ALU.add), p, accs[(c, j)], t_c)
                    accs[(c, j)] = bk.free

            prev = None
            order = [(c, e) for c in range(8) for e in range(8)]
            for idx, (c, e) in enumerate(order):
                if has_bias and e == 0:
                    bk = bank[6 + c % 2]
                    for j in range(4):
                        p = q.pe(lambda en, j=j, c=c, bk=bk: en.transpose(bk.t[0:8, 128 * j:128 * j + 128],
                                                                         cc[:, 4 * c + j, :], identf[:, :]), t_c, bk.free)
                    x = q.act(lambda en, c=c, bk=bk: en.activation(ctt[:, c % 2, :], bk.t[0:8, :], ACT.Copy), p)
                    for j in range(4):
                        p = q.pe(lambda en, j=j, c=c, bk=bk: en.matmul(bk.t[:, 128 * j:128 * j + 128],
                                                                       ctt[:, c % 2, 128 * j:128 * j + 128], b2s[:, :],
                                                                       start=True, stop=True), x, t_ct)
                    o = W[:, 4 * c:4 * c + 4, :].rearrange("p a b -> p (a b)")
                    bk.free = q.dve(lambda en, o=o, bk=bk: en.tensor_copy(o, bk.t[:, :]), p)
                    for j in range(4):
                        accs[(c, j)] = bk.free
                ht = []
                war = t_y.get(order[idx - 2]) if idx >= 2 else None
                for f in range(nf):
                    bk = bh[hc % 4]
                    hc += 1
                    p = q.pe(lambda en, bk=bk, f=f, e=e, c=c: en.matmul(
                        bk.t[:, :], W1[:, 128 * (e * nf + f):128 * (e * nf + f) + 128], ZT[:, 512 * c:512 * c + 512],
                        start=True, stop=True), bk.free, t_w, t_zt)
                    k = (e % 2) * nf + f
                    kw = dict(bias=cols[:, 8 + e * nf + f:9 + e * nf + f]) if has_bias else {}
                    bk.free = q.act(lambda en, bk=bk, k=k, kw=kw: en.activation(PB[:, k, :], bk.t[:, :], func, **kw), p,
                                    war, t_cols)
                    ht.append(bk.free)
                if prev is not None:
                    down(*prev)
                prev = (c, e, ht)
            down(*prev)
            return [accs[(c, 3)] for c in range(8)]

        def dv(fn, *w):
            return q.dve(fn, *w)

        gv = [gs[:, i, :] for i in range(14)]

        t_w0 = [load("w", WT[:, 0:640], ins["w_l0"])]
        t_m0 = [load("m", W1[:, 0:2048], ins["L0w1"]), load("m", W2[:, 0:2048], ins["L0w2"]), load("m", b2s[:, :], ins["L0b2"])]
        tz = []
        for b in range(B):
            r = ln_stats(X, b)
            z = ln_apply(Z, X, b, r)
            tz += transposed(Z, b, z, ZT)
        attention(0, WT[:, 0:128], WT[:, 128:256], WT[:, 256:384], cols[:, 4:5], cols[:, 5:6], bc[:, 1, :], None, t_w0, tz)
        ty = project(WT[:, 384:512], t_w0, Z, Z, 2)
        q.barrier()
        tz, t_yt = [], []
        for b in range(B):
            r = ln_stats(Z, b, ty[b])
            z = ln_apply(Z, Z, b, r)
            zs = Z[:, 8 * b:8 * b + 8, :]
            p1 = q.pool(lambda e, zs=zs: e.tensor_tensor(zs, zs, bc[:, 3:4, :].broadcast_to((128, 8, 128)), ALU.mult), z, t_bc)
            p2 = q.pool(lambda e, zs=zs: e.tensor_tensor(zs, zs, bc[:, 4:5, :].broadcast_to((128, 8, 128)), ALU.add), p1)
            t_yt.append(p2)
            tz += transposed(Z, b, p2, ZT)
        bk = bank[5]
        for t in range(NT):
            p = q.pe(lambda e, t=t: e.matmul(bk.t[:, 12 * t:12 * t + 12], ZT[:, 128 * t:128 * t + 128], WT[:, 512:524],
                                             start=True, stop=True), tz)
        gb = cols_gb = sb("gb", [128, 20])
        t_gb = load("gb", gb[:, :], ins["gate_b"].partition_broadcast(128))
        idx = sb("idx", [128, 8])
        t_idx = load("idx", idx[:, :], ins["idx"].partition_broadcast(128))
        lg = PB[:, 11, 0:384].rearrange("p (t k) -> p t k", k=12)
        a = dv(lambda e: e.tensor_tensor(lg[:, :, :], bk.t[:, 0:384].rearrange("p (t k) -> p t k", k=12),
                                         gb[:, 0:12].unsqueeze(1).broadcast_to((128, NT, 12)), ALU.add), p, t_gb)
        bk.free = a

        def v3(i, k):
            return gs[:, i, 0:NT * k].rearrange("p (t k) -> p t k", k=k)

        def first_max(lgv, mxi, k, w):
            m = gs[:, mxi + 1, 0:NT]
            a1 = dv(lambda e: e.tensor_reduce(m, lgv, AX.X, ALU.max), w)
            mb = m.unsqueeze(2).broadcast_to((128, NT, k))
            oh = v3(mxi, k)
            a2 = dv(lambda e: e.tensor_tensor(oh, lgv, mb, ALU.is_equal), a1)
            a3 = dv(lambda e: e.tensor_tensor(oh, oh, idx[:, 0:k].unsqueeze(1).broadcast_to((128, NT, k)), ALU.mult), a2, t_idx)
            c = gs[:, mxi + 2, 0:NT]
            a4 = dv(lambda e: e.tensor_reduce(c, oh, AX.X, ALU.max), a3)
            return dv(lambda e: e.tensor_tensor(oh, oh, c.unsqueeze(2).broadcast_to((128, NT, k)), ALU.is_equal), a4), a1

        lgv = lg[:, :, 0:4]
        t_oh, _ = first_max(lgv, 1, 4, a)
        gx = v3(4, 4)
        a = dv(lambda e: e.tensor_tensor(gx, lgv, gs[:, 2, 0:NT].unsqueeze(2).broadcast_to((128, NT, 4)), ALU.subtract), t_oh)
        a = q.act(lambda e: e.activation(gx, gx, ACT.Exp), a)
        gsum = gs[:, 5, 0:NT]
        a = dv(lambda e: e.tensor_reduce(gsum, gx, AX.X, ALU.add), a)
        l0 = lg[:, :, 4:8]
        l1 = lg[:, :, 8:12]
        em, x0, x1, f1, es = v3(6, 4), v3(7, 4), v3(8, 4), v3(9, 4), v3(10, 4)
        b1 = dv(lambda e: e.tensor_tensor(em, l0, l1, ALU.max), a)
        b2 = dv(lambda e: e.tensor_tensor(x0, l0, em, ALU.subtract), b1)
        b3 = dv(lambda e: e.tensor_tensor(x1, l1, em, ALU.subtract), b1)
        b4 = q.act(lambda e: e.activation(x0, x0, ACT.Exp), b2)
        b5 = q.act(lambda e: e.activation(x1, x1, ACT.Exp), b3)
        b6 = dv(lambda e: e.tensor_tensor(f1, l1, l0, ALU.is_gt), a)
        b7 = dv(lambda e: e.tensor_tensor(es, x0, x1, ALU.add), b4, b5)
        b8 = dv(lambda e: e.tensor_tensor(es, es, gsum.unsqueeze(2).broadcast_to((128, NT, 4)), ALU.mult), b7)
        b9 = dv(lambda e: e.reciprocal(es, es), b8)
        b10 = dv(lambda e: e.tensor_tensor(es, es, v3(1, 4), ALU.mult), b9)
        cc = gs[:, 0, :].rearrange("p (t g k) -> p t g k", g=4, k=2)
        b11 = dv(lambda e: e.tensor_tensor(cc[:, :, :, 1], es, f1, ALU.mult), b10, b6)
        b12 = dv(lambda e: e.tensor_tensor(cc[:, :, :, 0], es, cc[:, :, :, 1], ALU.subtract), b11)
        ta = moe(2, ACT.Relu, t_m0, b12, tz, t_m0, True)
        tr = []
        for b in range(B):
            zs = Z[:, 8 * b:8 * b + 8, :]
            ws = W[:, 8 * b:8 * b + 8, :]
            xs = X[:, 8 * b:8 * b + 8, :]
            a = dv(lambda e, zs=zs, ws=ws: e.tensor_tensor(zs, zs, ws, ALU.add), ta[2 * b:2 * b + 2])
            r = ln_stats(Z, b, a)
            z = ln_apply(Z, Z, b, r)
            p1 = q.pool(lambda e, zs=zs: e.tensor_tensor(zs, zs, bc[:, 5:6, :].broadcast_to((128, 8, 128)), ALU.mult), z)
            g2 = W[:, 8 * b:8 * b + 8, :]
            p2 = q.pool(lambda e, zs=zs, xs=xs: e.tensor_tensor(xs, xs, zs, ALU.add), p1)
            tr.append(p2)
        q.barrier()
        t_bc2 = load("bc2", bc[:, 0:1, :], ins["rows2"].partition_broadcast(128))
        for b in range(B):
            xs = X[:, 8 * b:8 * b + 8, :]
            tr[b] = q.pool(lambda e, xs=xs: e.tensor_tensor(xs, xs, bc[:, 0:1, :].broadcast_to((128, 8, 128)), ALU.add), t_bc2)

        t_wl = load("w", WT[:, 0:896], ins["w_l1"])
        t_rt = load("rt", W1[0:64, 0:2048], ins["rope"])
        bk = bank[0]
        p = q.pe(lambda e: e.matmul(bk.t[:, 0:320], WT[:, 0:128], WT[:, 128:448], start=True, stop=True), t_wl)
        WF = WT[:, 896:1216]
        f1_ = q.act(lambda e: e.activation(WF, bk.t[:, 0:320], ACT.Copy), p)
        rp0, rp1 = WT[:, 1216:1280], WT[:, 1280:1344]
        f2 = [q.dve(lambda e: e.tensor_copy(rp0[:, 0:32], WT[:, 576:608]), t_wl),
              q.dve(lambda e: e.tensor_copy(rp0[:, 32:64], WF[:, 256:288]), f1_),
              q.dve(lambda e: e.tensor_copy(rp1[:, 0:32], WT[:, 608:640]), t_wl),
              q.dve(lambda e: e.tensor_copy(rp1[:, 32:64], WF[:, 288:320]), f1_)]
        tz = []
        for b in range(B):
            r = ln_stats(X, b, tr[b])
            z = ln_apply(Z, X, b, r)
            tz += transposed(Z, b, z, ZT)
        OS2 = PB[:, 10, :]
        attention(1, WT[:, 448:576], WF[:, 0:128], WF[:, 128:256], cols[:, 6:7], cols[:, 6:7], None, (rp0, rp1),
                  [t_wl, f1_, f2, t_rt], tz)
        tx = project(WT[:, 640:768], t_wl, X, X, None)
        q.barrier()

        t_w3 = load("w", WT[:, 0:520], ins["w_l2"])
        t_m3 = [load("m", W1[:, :], ins["L1w1"]), load("m", W2[:, :], ins["L1w2"])]
        tz = []
        for b in range(B):
            r = ln_stats(X, b, tx[b])
            z = ln_apply(Z, X, b, r)
            r2 = ln_stats(Z, b, z)
            z2 = ln_apply(W, Z, b, r2)
            tz += transposed(W, b, z2, ZT, scale=cols[:, 24:25], bias=cols[:, 25:26])
        attention(2, WT[:, 0:128], WT[:, 128:256], WT[:, 256:384], cols[:, 6:7], cols[:, 6:7], None, None, t_w3, tz)
        ty = project(WT[:, 384:512], t_w3, Z, Z, None)
        q.barrier()
        tz = []
        for b in range(B):
            r = ln_stats(Z, b, ty[b])
            z = ln_apply(W, Z, b, r)
            tz += transposed(W, b, z, ZT, scale=cols[:, 26:27], bias=cols[:, 27:28])
            zs, xs = Z[:, 8 * b:8 * b + 8, :], X[:, 8 * b:8 * b + 8, :]
            tr[b] = q.pool(lambda e, zs=zs, xs=xs: e.tensor_tensor(xs, xs, zs, ALU.add), ty[b])
        bk = bank[5]
        for t in range(NT):
            p = q.pe(lambda e, t=t: e.matmul(bk.t[:, 8 * t:8 * t + 8], ZT[:, 128 * t:128 * t + 128], WT[:, 512:520],
                                             start=True, stop=True), tz)
        l8 = gs[:, 7, :].rearrange("p (t k) -> p t k", k=8)
        a = dv(lambda e: e.tensor_tensor(l8, bk.t[:, 0:256].rearrange("p (t k) -> p t k", k=8),
                                         gb[:, 12:20].unsqueeze(1).broadcast_to((128, NT, 8)), ALU.add), p)
        bk.free = a
        t_oh, _ = first_max(l8, 1, 8, a)
        a = dv(lambda e: e.tensor_copy(gs[:, 0, :], gs[:, 1, :]), t_oh)
        ta = moe(4, ACT.Gelu_apprx_tanh, t_m3, a, tz, None, False)
        od = out.rearrange("(t p) d -> p t d", p=128)
        outs = []
        for c in range(8):
            xs = X[:, 4 * c:4 * c + 4, :]
            a = dv(lambda e, xs=xs, c=c: e.tensor_tensor(xs, xs, W[:, 4 * c:4 * c + 4, :], ALU.add), ta[c], tr[c // 2])
            outs.append(q.dma("o", od[:, 4 * c:4 * c + 4, :], xs, a))
        q.finish([t for t in q.dma_open])
        block = ctx.enter_context(nc.Block())
        q.emit(block)


def kernel(**I):
    import numpy as _np
    import ml_dtypes
    import concourse.bacc as _bacc
    from concourse import mybir as _mybir
    from concourse.bass_utils import run_bass_kernel_spmd as _run

    f32 = _np.float32
    I = {k: _np.asarray(v) for k, v in I.items()}

    def chunks(a):
        n = a.shape[0] // 128
        return _np.concatenate([a[128 * c:128 * c + 128] for c in range(n)], axis=1)

    def rep4(a):
        z = _np.zeros((a.shape[0], 16), f32)
        return _np.concatenate([a, z] * 4, axis=1)

    def swap(a):
        return _np.concatenate([a[:, 16:32], a[:, 0:16]], axis=1)

    eye = _np.eye(128, dtype=f32)
    z1 = _np.zeros((128, 1), f32)
    cols = [I["L0_attn_norm_w"][:, None], I["L0_attn_norm_b"][:, None],
            I["L0_attn_b_in"][0:128, None], I["L0_attn_b_in"][128:256, None],
            I["L0_ffn_in_proj_b"][0:128, None], I["L0_ffn_in_proj_b"][128:256, None], z1, z1,
            I["L0_ffn_b1"].reshape(16, 128).T,
            I["L1_ffn_ln1_w"][:, None], I["L1_ffn_ln1_b"][:, None], I["L1_ffn_ln2_w"][:, None], I["L1_ffn_ln2_b"][:, None]]
    cols = _np.concatenate(cols, axis=1)
    cols = _np.concatenate([cols, _np.zeros((128, 40 - cols.shape[1]), f32)], axis=1)
    rows = _np.stack([I["L0_attn_b_out"], I["L0_ffn_in_proj_b"][256:384], I["L0_ffn_out_proj_b"],
                      I["L0_ffn_ln1_g"], I["L0_ffn_ln1_b"], I["L0_ffn_ln2_g"]])
    kk, qq = _np.meshgrid(_np.arange(128), _np.arange(128), indexing="ij")
    m_max = _np.where(qq > kk, NEG, 0.0)
    m_all = _np.full((128, 128), NEG)
    m_main = _np.where(kk > qq, NEG, 0.0)
    mask = _np.concatenate([m_max, m_all, m_main], axis=1).astype(ml_dtypes.bfloat16)
    sel = _np.zeros((128, 18), f32)
    for j in range(4):
        for r in range(9):
            sel[32 * j + r, 9 * (j % 2) + r] = 1.0
    w_ssm = _np.concatenate([chunks(I["L0_attn_W_in"]), chunks(rep4(I["L0_attn_A"])), chunks(rep4(I["L0_attn_B_ssm"])),
                             chunks(rep4(I["L0_attn_C_ssm"])), chunks(I["L0_attn_W_out"].T)], axis=1)
    w_l0 = _np.concatenate([I["L0_ffn_in_proj_w"].T, I["L0_ffn_out_proj_w"].T, I["L0_ffn_w_group"],
                            I["L0_ffn_w_expert"][:, :, 0].T, I["L0_ffn_w_expert"][:, :, 1].T,
                            _np.zeros((128, 116), f32)], axis=1)
    w_l1 = _np.concatenate([I["L1_attn_W_kv_down"].T, I["L1_attn_W_k_up"], I["L1_attn_W_v_up"], I["L1_attn_W_k_rope"],
                            swap(I["L1_attn_W_k_rope"]), I["L1_attn_W_q"], I["L1_attn_W_q_rope"],
                            swap(I["L1_attn_W_q_rope"]), I["L1_attn_W_o"], _np.zeros((128, 128), f32)], axis=1)
    w_l2 = _np.concatenate([I["L1_ffn_w_qkv"], I["L1_ffn_w_proj"], I["L1_ffn_gate_w"]], axis=1)
    inv = (f32(1.0) / _np.power(f32(10000.0), _np.arange(0, 32, 2, dtype=f32) / f32(32))).astype(f32)
    fr = _np.outer(_np.arange(S, dtype=f32), inv).astype(f32).T
    cs, sn = _np.cos(fr), _np.sin(fr)
    rope = _np.concatenate([_np.concatenate([cs, cs, cs, cs]), _np.concatenate([-sn, sn, -sn, sn])], axis=1).astype(f32)
    be = I["L0_ffn_b_expert"]
    arrays = {
        "x": I["L0_attn_x"].reshape(B * S, D), "cols": cols, "rows": rows, "rows2": I["L0_ffn_ln2_b"][None, :],
        "identf": eye, "identb": eye.astype(ml_dtypes.bfloat16), "maskb": mask, "sel": sel,
        "ones": _np.ones((3, 1024), ml_dtypes.bfloat16), "zeros": _np.zeros((3, 1024), ml_dtypes.bfloat16),
        "idx": _np.arange(8, 0, -1).astype(f32),
        "gate_b": _np.concatenate([I["L0_ffn_b_group"], be[:, 0], be[:, 1], I["L1_ffn_gate_b"]]),
        "w_ssm": w_ssm, "w_l0": w_l0, "w_l1": w_l1, "w_l2": w_l2, "rope": rope,
        "L0w1": I["L0_ffn_w1"].transpose(1, 0, 2).reshape(128, 2048),
        "L0w2": I["L0_ffn_w2"].reshape(8, 2, 128, 128).transpose(2, 0, 1, 3).reshape(128, 2048),
        "L0b2": I["L0_ffn_b2"],
        "L1w1": I["L1_ffn_w1"].transpose(1, 0, 2).reshape(128, 4096),
        "L1w2": I["L1_ffn_w2"].reshape(8, 4, 128, 128).transpose(2, 0, 1, 3).reshape(128, 4096),
    }
    nc = _bacc.Bacc("TRN2", target_bir_lowering=False, num_devices=1)
    feed, aps = {}, {}
    for name, a in arrays.items():
        a = _np.ascontiguousarray(a)
        feed[f"in_{name}"] = a
        aps[name] = nc.dram_tensor(f"in_{name}", a.shape, _mybir.dt.from_np(a.dtype), kind="ExternalInput").ap()
    out = nc.dram_tensor("out_0", (B * S, D), F32, kind="ExternalOutput").ap()
    build(nc, aps, out)
    r = _run(nc, [feed], core_ids=[0])
    return r.results[0]["out_0"].reshape(B, S, D)
```

```python
from contextlib import ExitStack

import numpy as np
import concourse.bass as bass
from concourse import mybir

F32 = mybir.dt.float32
BF16 = mybir.dt.bfloat16
ACT = mybir.ActivationFunctionType
ALU = mybir.AluOpType
AX = mybir.AxisListType

B, S, D = 4, 1024, 128
NT = 32
TB = 8
H, HD = 16, 8
UNITS = B * H
EPS = 1e-5
NEG = -1.0e30


class Tok:

    def __init__(self, eng):
        self.eng, self.need, self.sem, self.val = eng, False, None, 0


class Queues:

    ENG = ("tensor", "scalar", "vector", "gpsimd", "sync")

    def __init__(self, nc, ctx):
        self.nc, self.ctx = nc, ctx
        self.q = {e: [] for e in self.ENG}
        self.last = {e: None for e in self.ENG}
        self.dma_n = {}
        self.dma_sems = {}
        self.dma_open = []

    def op(self, eng, fn, *waits):
        t = Tok(eng)
        self.q[eng].append((self.flat(waits), fn, t))
        self.last[eng] = t
        return t

    def pe(self, fn, *w):
        return self.op("tensor", fn, *w)

    def act(self, fn, *w):
        return self.op("scalar", fn, *w)

    def dve(self, fn, *w):
        return self.op("vector", fn, *w)

    def pool(self, fn, *w):
        return self.op("gpsimd", fn, *w)

    def flat(self, waits):
        out = []
        for w in waits:
            if isinstance(w, Tok):
                w.need = True
                out.append(w)
            elif w:
                out.extend(self.flat(w))
        return out

    def dma(self, stream, dst, src, *waits, eng="sync"):
        n = self.dma_n.get(stream, 0)
        self.dma_n[stream] = n + 1
        if stream not in self.dma_sems:
            self.dma_sems[stream] = self.ctx.enter_context(self.nc.semaphore("d_" + stream))
        t = Tok("dma")
        t.need, t.sem, t.val = True, self.dma_sems[stream], 16 * (n + 1)
        self.q[eng].append((self.flat(waits), lambda e: e.dma_start(dst, src), t))
        self.dma_open.append(t)
        return t

    def barrier(self, *extra):
        ends = [self.last[e] for e in ("tensor", "scalar", "vector", "gpsimd") if self.last[e] is not None]
        for e in self.ENG:
            self.q[e].append((self.flat([ends, extra]), None, None))
        return ends

    def finish(self, toks):
        self.q["sync"].append((self.flat([toks]), None, None))

    def emit(self, block):
        for e in ("tensor", "scalar", "vector", "gpsimd"):
            sem = self.ctx.enter_context(self.nc.semaphore("s_" + e))
            n = 0
            for _, _, t in self.q[e]:
                if t is not None and t.eng == e and t.need:
                    n += 1
                    t.sem, t.val = sem, n

        def program(name):
            def run(eng):
                seen = {}
                for waits, fn, t in self.q[name]:
                    best = {}
                    for w in waits:
                        if w.val > best.get(id(w.sem), (None, 0))[1]:
                            best[id(w.sem)] = (w.sem, w.val)
                    for k, (s, v) in best.items():
                        if seen.get(k, 0) < v:
                            eng.wait_ge(s, v)
                            seen[k] = v
                    if fn is None:
                        continue
                    ins = fn(eng)
                    if t.eng == "dma":
                        ins.then_inc(t.sem, 16)
                    elif t.need:
                        ins.then_inc(t.sem, 1)
            return run

        block.tensor(program("tensor"))
        block.scalar(program("scalar"))
        block.vector(program("vector"))
        block.gpsimd(program("gpsimd"))
        block.sync(program("sync"))


class Bank:

    def __init__(self, t):
        self.t, self.free = t, None


def build(nc, ins, out):
    with ExitStack() as ctx:
        q = Queues(nc, ctx)

        def sb(name, shape, dt=F32):
            return ctx.enter_context(nc.sbuf_tensor(name, shape, dt))

        X = sb("X", [128, NT, 128])
        Z = sb("Z", [128, NT, 128])
        W = sb("W", [128, NT, 128])
        ZT = sb("ZT", [128, NT * 128])
        VP = sb("VP", [128, NT, 168])
        PB = sb("PB", [128, 12, 512])
        NB = 4
        RK = sb("RK", [128, NB, 4, 1024], BF16)
        W1 = sb("W1", [128, 8 * 512])
        W2 = sb("W2", [128, 8 * 4 * 128])
        OS = sb("OS", [128, 2, 512])
        WT = sb("WT", [128, 1920])
        identf = sb("identf", [128, 128])
        identb = sb("identb", [128, 128], BF16)
        maskb = sb("maskb", [128, 256], BF16)
        bc = sb("bc", [128, 6, 128])
        cols = sb("cols", [128, 40])
        st = sb("st", [128, NT, 6])
        mv = sb("mv", [128, NT, 2])
        rs = sb("rs", [128, 4, NT])
        small = sb("small", [128, 4, 64])
        nms = sb("nms", [24, 4, 128], BF16)
        gs = sb("gs", [128, 14, NT * 8])
        ctt = OS[0:8, :, :]
        b2s = sb("b2s", [8, 128])
        bank = [Bank(ctx.enter_context(nc.psum_tensor(f"bank{i}", [128, 512], F32))) for i in range(8)]
        QD = nc.dram_tensor("q_parts", (B, 5, 128, 1024), BF16, kind="Internal").ap()
        KD = nc.dram_tensor("k_parts", (B, 5, 128, 1024), BF16, kind="Internal").ap()
        RQD = nc.dram_tensor("rq_parts", (B, 5, 32, 1024), BF16, kind="Internal").ap()
        RKD = nc.dram_tensor("rk_parts", (B, 5, 32, 1024), BF16, kind="Internal").ap()

        def load(stream, dst, src, *w, eng="sync"):
            return q.dma(stream, dst, src, *w, eng=eng)

        xin = ins["x"].rearrange("(t p) d -> p t d", p=128)
        tx = [q.dma("x%d" % b, X[:, 8 * b:8 * b + 8, :], xin[:, 8 * b:8 * b + 8, :]) for b in range(B)]
        t_cols = load("c_cols", cols[:, :], ins["cols"], eng="scalar")
        t_idf = load("c_idf", identf[:, :], ins["identf"], eng="scalar")
        t_idb = load("c_idb", identb[:, :], ins["identb"], eng="scalar")
        t_mask = load("c_mask", maskb[:, :], ins["maskb"], eng="scalar")
        t_bc = load("c_bc", bc[:, :, :], ins["rows"].partition_broadcast(128), eng="scalar")
        wssm = WT[:, 0:1280]
        t_ws = load("c_ws", wssm, ins["w_ssm"], eng="scalar")

        def ln_stats(src, b, *w):
            lo, hi = 8 * b, 8 * b + 8
            a = [q.dve(lambda e, t=t: e.bn_stats(st[:, t, :], src[:, t, :]), *w) for t in range(lo, hi)]
            g = [q.dve(lambda e, t=t: e.bn_aggr(mv[:, t, :], st[:, t, :]), a[t - lo]) for t in range(lo, hi)]
            ve, sd, r, n = (rs[:, i, lo:hi] for i in range(4))
            t1 = q.dve(lambda e: e.tensor_scalar(ve, mv[:, lo:hi, 1], EPS, None, ALU.add), g[-1])
            t2 = q.act(lambda e: e.activation(sd, ve, ACT.Sqrt), t1)
            t3 = q.dve(lambda e: e.reciprocal(r, sd), t2)
            t4 = q.dve(lambda e: e.tensor_tensor(n, r, r, ALU.mult), t3)
            t5 = q.dve(lambda e: e.tensor_tensor(n, n, ve, ALU.mult), t4)
            t6 = q.dve(lambda e: e.tensor_scalar(n, n, -0.5, 1.5, ALU.mult, ALU.add), t5)
            return q.dve(lambda e: e.tensor_tensor(r, r, n, ALU.mult), t6)

        def ln_apply(dst, src, b, t_r):
            for t in range(8 * b, 8 * b + 8):
                k = q.dve(lambda e, t=t: e.tensor_scalar(dst[:, t, :], src[:, t, :], mv[:, t, 0:1], rs[:, 2, t:t + 1],
                                                         ALU.subtract, ALU.mult), t_r)
            return k

        def transposed(src, b, t_src, dst, scale=None, bias=None, pair=(6, 7)):
            toks = []
            for c in range(2 * b, 2 * b + 2):
                bk = bank[pair[c % 2]]
                for j in range(4):
                    p = q.pe(lambda e, j=j, c=c, bk=bk: e.transpose(bk.t[:, 128 * j:128 * j + 128], src[:, 4 * c + j, :],
                                                                    identf[:, :]), t_src, bk.free, t_idf)
                o = dst[:, 512 * c:512 * c + 512]
                if scale is None:
                    bk.free = q.act(lambda e, o=o, bk=bk: e.activation(o, bk.t[:, :], ACT.Copy), p)
                else:
                    bk.free = q.act(lambda e, o=o, bk=bk: e.activation(o, bk.t[:, :], ACT.Identity, bias=bias,
                                                                       scale=scale), p, t_cols)
                toks.append(bk.free)
            return toks

        t_ssm_in = []
        t_z0 = []
        for b in range(B):
            r = ln_stats(X, b, tx[b])
            z = ln_apply(Z, X, b, r)
            t_z0.append(z)
            r2 = ln_stats(Z, b, z)
            z2 = ln_apply(W, Z, b, r2)
            t_ssm_in += transposed(W, b, z2, ZT, scale=cols[:, 0:1], bias=cols[:, 1:2])
        w_in = wssm[:, 0:256].rearrange("p (c n) -> p c n", c=2)
        a_rep = wssm[:, 256:512].rearrange("p (c n) -> p c n", c=2)
        b_rep = wssm[:, 512:768].rearrange("p (c n) -> p c n", c=2)
        c_rep = wssm[:, 768:1024].rearrange("p (c n) -> p c n", c=2)
        wo_t = wssm[:, 1024:1280].rearrange("p (c n) -> p c n", c=2)
        gsb = WT[:, 1280:1344]
        h4 = WT[:, 1344:1472]
        bb = cols[:, 36:40]
        bk = bank[0]
        for c in range(2):
            q.pe(lambda e, c=c: e.matmul(bk.t[:, 0:32], w_in[:, c, :], a_rep[:, c, 0:32], start=(c == 0), stop=(c == 1)), t_ws)
        for c in range(2):
            p = q.pe(lambda e, c=c: e.matmul(bk.t[:, 32:64], w_in[:, c, :], b_rep[:, c, 0:32], start=(c == 0), stop=(c == 1)))
        t_g = q.act(lambda e: e.activation(gsb, bk.t[:, 0:64], ACT.Copy), p)
        bk1 = bank[1]
        for c in range(2):
            p = q.pe(lambda e, c=c: e.matmul(bk1.t[:, 0:128], c_rep[:, c, :], wo_t[:, c, :], start=(c == 0), stop=(c == 1)))
        t_h = q.act(lambda e: e.activation(h4, bk1.t[:, 0:128], ACT.Copy), p)
        bk2 = bank[2]
        for i, rep in enumerate((a_rep, b_rep)):
            for c in range(2):
                p = q.pe(lambda e, c=c, i=i, rep=rep: e.matmul(bk2.t[:, i:i + 1], rep[:, c, :], cols[:, 2 + c:3 + c],
                                                               start=(c == 0), stop=(c == 1)), t_cols)
        t_b1 = q.dve(lambda e: e.tensor_scalar(bb[:, 0:1], bk2.t[:, 0:1], -1.0, None, ALU.mult), p)
        t_b2 = q.dve(lambda e: e.tensor_copy(bb[:, 1:2], bk2.t[:, 1:2]), p)
        q.barrier()
        A_s, U_s, S_s = PB[:, 0:2, :], PB[:, 2:4, :], PB[:, 4:6, :]
        pa = []
        for i, base in ((0, 2), (1, 4)):
            for hf in range(2):
                for b in range(B):
                    p = q.pe(lambda e, i=i, base=base, hf=hf, b=b: e.matmul(
                        bank[base + hf].t[32 * b:32 * b + 32, :], gsb[:, 32 * i:32 * i + 32],
                        ZT[:, 1024 * b + 512 * hf:1024 * b + 512 * hf + 512], start=True, stop=True), t_g)
                pa.append(p)
        ta = []
        for hf in range(2):
            x = q.act(lambda e, hf=hf: e.activation(A_s[:, hf, :], bank[2 + hf].t[:, :], ACT.Exp, bias=bb[:, 0:1],
                                                    scale=-1.0), pa[hf], t_b1)
            y = q.dve(lambda e, hf=hf: e.tensor_scalar(A_s[:, hf, :], A_s[:, hf, :], 1.0, None, ALU.add), x)
            ta.append(q.dve(lambda e, hf=hf: e.reciprocal(A_s[:, hf, :], A_s[:, hf, :]), y))
            tu = q.act(lambda e, hf=hf: e.activation(U_s[:, hf, :], bank[4 + hf].t[:, :], ACT.Identity, bias=bb[:, 1:2]),
                       pa[2 + hf], t_b2)
            ta.append(tu)
        t_scan = q.dve(lambda e: e.tensor_tensor_scan(S_s.rearrange("p a b -> p (a b)"), A_s.rearrange("p a b -> p (a b)"),
                                                      U_s.rearrange("p a b -> p (a b)"), 0.0, ALU.mult, ALU.add), ta)
        t_x = []
        for b in range(B):
            zs = Z[:, 8 * b:8 * b + 8, :]
            p1 = q.pool(lambda e, zs=zs: e.tensor_tensor(zs, zs, bc[:, 0:1, :].broadcast_to((128, 8, 128)), ALU.add), t_bc)
            xs = X[:, 8 * b:8 * b + 8, :]
            t_x.append(q.pool(lambda e, xs=xs, zs=zs: e.tensor_tensor(xs, xs, zs, ALU.add), p1))
        sv = S_s.rearrange("p a b -> p (a b)")
        for c in range(8):
            b = c // 2
            bk = bank[c % 2]
            for j in range(4):
                tt = (4 * c + j) % 8
                p = q.pe(lambda e, b=b, bk=bk, j=j, tt=tt: e.matmul(
                    bk.t[:, 128 * j:128 * j + 128], sv[32 * b:32 * b + 32, 128 * tt:128 * tt + 128],
                    h4[32 * b:32 * b + 32, :], start=True, stop=True), t_scan, t_h, bk.free if c > 1 else None)
            xs = X[:, 4 * c:4 * c + 4, :].rearrange("p a b -> p (a b)")
            bk.free = q.dve(lambda e, xs=xs, bk=bk: e.tensor_tensor(xs, xs, bk.t[:, :], ALU.add), p, t_x[b])
            t_x[b] = bk.free
        q.barrier()

        t_vz = q.pool(lambda e: e.memset(VP[:, :, 144:168], 0.0))
        VH = VP[:, :, 0:144].rearrange("p t (h c) -> p t h c", c=9)
        t_vo = q.pool(lambda e: e.memset(VH[:, :, :, 8:9], 1.0))

        def attention(layer, wq, wk, wv, qb, kb, vb, wrope, t_w, t_zt):
            causal = layer == 1
            scale = 1.0 / float(np.sqrt(40.0 if causal else 8.0))
            for bkk in bank:
                bkk.free = None
            wr = {}
            tmp = PB
            nslot = [0]

            if causal:
                q_seq = ((0, 2), (1, 3), (4,))
                k_seq = ((2, 3), (1, 4), (0,))
            else:
                q_seq = ((0, 3), (1, 4), (2,))
                k_seq = ((0,), (1,), (2,))

            def parts(pt, rows, bias, dst, c, extra=None):
                s = nslot[0] % 3
                n = nslot[0]
                nslot[0] += 1
                prev = slot_done[s]
                x = tmp[0:rows, 3 * s, :]
                r1 = tmp[0:rows, 3 * s + 1, :]
                sp = tmp[0:rows, 3 * s + 2, :].bitcast(BF16)
                sp3 = lo3[0:rows, s, :]
                hi, mid, lo = sp[:, 0:512], sp[:, 512:1024], sp3
                bkk, p = pt
                if extra is None:
                    x1 = q.act(lambda e: e.activation(x, bkk.t[0:rows, :], ACT.Identity, bias=bias), p, prev, t_cols)
                    bkk.free = x1
                else:
                    x1 = extra(x, prev)
                h1 = q.dve(lambda e: e.tensor_copy(hi, x), x1, prev)
                d1 = q.dve(lambda e: e.tensor_tensor(r1, x, hi, ALU.subtract), h1)
                d2 = q.dve(lambda e: e.tensor_copy(mid, r1), d1)
                d3 = q.dve(lambda e: e.tensor_tensor(lo, r1, mid, ALU.subtract), d2)
                b, tc = c // 2, slice(512 * (c % 2), 512 * (c % 2) + 512)
                ds = []
                for k, src in enumerate((hi, mid, lo)):
                    for dd, r0, nr, seq in dst:
                        for m in seq[k]:
                            ds.append(q.dma("sc%d" % s, dd[b, m, :, tc], src[r0:r0 + nr, :], d3))
                slot_done[s] = ds
                wr.setdefault(b, []).extend(ds)

            slot_done = [None] * 3
            lo3 = OS[:, :, :].rearrange("p a b -> p (a b)").bitcast(BF16)[:, 0:1536].rearrange("p (s n) -> p s n", s=3)
            kk = 0
            for c in range(8):
                for wt, bias, dst in ((wq, qb, [(QD, 0, 128, q_seq)]), (wk, kb, [(KD, 0, 128, k_seq)])):
                    bkk = bank[kk % 4]
                    kk += 1
                    p = q.pe(lambda e, bkk=bkk, wt=wt, c=c: e.matmul(bkk.t[:, :], wt, ZT[:, 512 * c:512 * c + 512],
                                                                     start=True, stop=True), bkk.free, t_w, t_zt)
                    parts((bkk, p), 128, bias, dst, c)
                if causal:
                    b0, b1 = bank[4], bank[5]
                    p0 = q.pe(lambda e, c=c: e.matmul(b0.t[0:64, :], wrope[0], ZT[:, 512 * c:512 * c + 512], start=True,
                                                      stop=True), b0.free)
                    p1 = q.pe(lambda e, c=c: e.matmul(b1.t[0:64, :], wrope[1], ZT[:, 512 * c:512 * c + 512], start=True,
                                                      stop=True), b1.free)

                    def rot(x, prev, c=c, p0=p0, p1=p1):
                        o = 512 * (c % 2)
                        m0 = q.dve(lambda e: e.tensor_tensor(x, b0.t[0:64, :], W1[0:64, o:o + 512], ALU.mult), p0, prev, t_w)
                        y = OS2[0:64, :]
                        m1 = q.dve(lambda e: e.tensor_tensor(y, b1.t[0:64, :], W1[0:64, 1024 + o:1536 + o], ALU.mult), p1)
                        b0.free, b1.free = m0, m1
                        return q.dve(lambda e: e.tensor_tensor(x, x, y, ALU.add), m1)
                    parts((b0, p0), 64, None, [(RQD, 0, 32, q_seq), (RKD, 32, 32, k_seq)], c, rot)
                bkk = bank[6 + c % 2]
                for j in range(4):
                    p = q.pe(lambda e, bkk=bkk, c=c, j=j: e.matmul(bkk.t[:, 128 * j:128 * j + 128],
                                                                   ZT[:, 512 * c + 128 * j:512 * c + 128 * j + 128], wv,
                                                                   start=True, stop=True), bkk.free)
                o = VH[:, 4 * c:4 * c + 4, :, 0:8]
                i0 = bkk.t[:, :].rearrange("p (t h c) -> p t h c", t=4, c=8)
                for j in range(4):
                    if vb is None:
                        bkk.free = q.act(lambda e, o=o, i0=i0, j=j: e.activation(o[:, j], i0[:, j], ACT.Copy), p)
                    else:
                        bkk.free = q.dve(lambda e, o=o, i0=i0, j=j: e.tensor_tensor(
                            o[:, j], i0[:, j], vb.rearrange("p (h c) -> p h c", c=8), ALU.add), p, t_bc)
            t_v = bkk.free
            q.barrier(slot_done)

            M0 = 96
            E0 = 104
            NS = 6 if causal else 8

            def slot(u, k, r0=0, r1=128):
                s = u % NS
                if not causal:
                    return RK[r0:r1, s // 2, 2 * (s % 2) + k, :]
                if s < 4:
                    return RK[r0:r1, s, k, :]
                return W2[r0:r1, 2048 * (s - 4) + 512 * k:2048 * (s - 4) + 512 * k + 512].bitcast(BF16)

            NK = 4 if causal else 2
            t_fill, ones_t = [], []
            for s in range(NS):
                t_fill.append([q.pool(lambda e, s=s, k=k: e.memset(slot(s, k), 0.0)) for k in range(NK)])
                ones_t.append(q.dma("ld%d" % s, slot(s, 1, M0, M0 + 3), ins["ones"], t_fill[s]))
            loaded = {}
            mained = {}
            maxed = {}

            def fetch(u):
                s, b, h = u % NS, u // H, u % H
                r = slice(8 * h, 8 * h + 8)
                w = [t_fill[s], ones_t[s], wr[b], mained.get(u - NS)]
                L = []

                def cp(k, row, src):
                    L.append(q.dma("ld%d" % s, slot(u, k, row, row + src.shape[0] * src.shape[1]), src, w))
                if causal:
                    cp(0, E0, QD[b, 0:3, r, :])
                    cp(1, E0, KD[b, 2:5, r, :])
                    cp(2, E0, QD[b, 2:5, r, :])
                    cp(3, E0, KD[b, 0:3, r, :])
                    if h < NS:
                        cp(0, 0, RQD[b, 0:3])
                        cp(1, 0, RKD[b, 2:5])
                        cp(2, 0, RQD[b, 2:5])
                        cp(3, 0, RKD[b, 0:3])
                else:
                    for i in range(3):
                        cp(0, 24 * i, QD[b, i:i + 3, r, :])
                        cp(1, 24 * i, KD[b, 0:3, r, :])
                if u >= NS:
                    L.append(q.pool(lambda e: e.memset(slot(u, 0, M0, M0 + 3), 0.0), mained[u - NS],
                                    q.last["gpsimd"]))
                loaded[u] = L

            if causal:
                mains = [(kt, hh, qh, max(0, 128 * kt - 512 * qh)) for kt in range(8) for hh in range(2)
                         for qh in range(kt // 4, 2)]
                maxes = [(qt, kh, min(512, 128 * (qt + 1) - 512 * kh)) for qt in range(8) for kh in range(qt // 4 + 1)]
                t_m2 = q.pool(lambda e: e.memset(small[:, 0:2, 0:16], NEG))
            else:
                mains = [(kt, hh, qh, 0) for kt in range(8) for hh in range(2) for qh in range(2)]
                maxes = [(qt, kh, 512) for qt in range(8) for kh in range(2)]
                t_m2 = None
            n, n2 = len(maxes), len(mains)
            assert n2 == 2 * n
            bmain, bmax, bav, bsel = bank[0:3], bank[3:6], bank[6], bank[7]
            t_nm, sent, t_exp, t_av, t_os = {}, {}, {}, {}, {}
            NPB = 12

            def max_step(u, i):
                qt, kh, wd = maxes[i]
                bkk = bmax[(u * n + i) % 3]
                diag = causal and kh == qt // 4
                w = loaded[u] if i == 0 else None
                p = q.pe(lambda e: e.matmul(bkk.t[:, 0:wd], slot(u, 0)[:, 128 * qt:128 * qt + 128],
                                            slot(u, 1)[:, 512 * kh:512 * kh + wd], start=True, stop=not diag), bkk.free, w)
                if diag:
                    p = q.pe(lambda e: e.matmul(bkk.t[:, wd - 128:wd], identb[:, :], maskb[:, 0:128], start=False,
                                                stop=True), t_idb, t_mask)
                m2 = small[:, u % 2, 0:16]
                bkk.free = q.dve(lambda e: e.tensor_reduce(m2[:, 2 * qt + kh:2 * qt + kh + 1], bkk.t[:, 0:wd], AX.X,
                                                           ALU.max), p, t_m2)
                if i == n - 1:
                    maxed[u] = bkk.free

            def max_end(u):
                k = u % 2
                m2, nm, r1 = small[:, k, 0:16], small[:, k, 16:24], small[:, k, 24:32]
                pts = small[:, 2 + k, 0:32].bitcast(BF16)
                a = q.dve(lambda e: e.tensor_reduce(nm, m2.rearrange("p (a b) -> p a b", b=2), AX.X, ALU.max, negate=True),
                          maxed[u])
                b_ = q.pool(lambda e: e.tensor_copy(pts[:, 0:8], nm), a, q.last["gpsimd"])
                c = q.pool(lambda e: e.tensor_tensor(r1, nm, pts[:, 0:8], ALU.subtract), b_)
                d = q.pool(lambda e: e.tensor_copy(pts[:, 8:16], r1), c)
                t_nm[u] = q.pool(lambda e: e.tensor_tensor(pts[:, 16:24], r1, pts[:, 8:16], ALU.subtract), d)

            def max_send(u):
                pts = small[:, 2 + u % 2, 0:32].bitcast(BF16)
                tb = bsel.t[0:24, 0:64].bitcast(BF16)
                p = q.pe(lambda e: e.transpose(tb, pts[:, 0:24], identb[:, :]), t_nm[u], bsel.free, t_idb)
                o = nms[:, u % 4, :]
                bsel.free = q.act(lambda e: e.activation(o, tb, ACT.Copy), p, sent.get(u - 4))
                sent[u] = q.dma("nm%d" % (u % 4), slot(u, 0, M0, M0 + 3).rearrange("p (t c) -> p t c", t=8), o,
                                bsel.free, loaded[u], maxed[u])

            def main_step(pr, i):
                kt, hh, qh, c0 = mains[i]
                u = 2 * pr + hh
                g = pr * n2 + i
                bkk = bmain[g % 3]
                w = sent[u] if kt == 0 else None
                qs = slice(512 * qh + c0, 512 * qh + 512)
                ks = slice(128 * kt, 128 * kt + 128)
                diag = causal and kt // 4 == qh
                p = q.pe(lambda e: e.matmul(bkk.t[:, c0:512], slot(u, 1)[:, ks], slot(u, 0)[:, qs], start=True,
                                            stop=not causal), bkk.free, w)
                if causal:
                    p = q.pe(lambda e: e.matmul(bkk.t[:, c0:512], slot(u, 3)[:, ks], slot(u, 2)[:, qs], start=False,
                                                stop=not diag))
                if diag:
                    p = q.pe(lambda e: e.matmul(bkk.t[:, c0:c0 + 128], identb[:, :], maskb[:, 128:256], start=False,
                                                stop=True))
                mained[u] = p
                o = PB[:, g % NPB, c0:512]
                bkk.free = q.act(lambda e: e.activation(o, bkk.t[:, c0:512], ACT.Exp, scale=scale), p,
                                 t_av.get(g - NPB))
                t_exp[g] = bkk.free

            def av_group(gg):
                for g in range(4 * gg, 4 * gg + 4):
                    pr, i = g // n2, g % n2
                    kt, hh, qh, c0 = mains[i]
                    b, h = pr // 8, 2 * (pr % 8) + hh
                    j = 2 * hh + qh
                    p = q.pe(lambda e, g=g, b=b, h=h, kt=kt, c0=c0, j=j, qh=qh: e.matmul(
                        bav.t[32 * j:32 * j + 32, c0:512], VP[:, 8 * b + kt, 9 * h:9 * h + 32], PB[:, g % NPB, c0:512],
                        start=(kt == 0), stop=(kt == (3 + 4 * qh if causal else 7))), t_exp[g], bav.free, t_v, t_vz, t_vo)
                    t_av[g] = p
                if (gg + 1) % (n2 // 4) == 0:
                    pr = (gg + 1) // (n2 // 4) - 1
                    o = OS[:, pr % 2, :]
                    bav.free = q.act(lambda e: e.activation(o, bav.t[:, :], ACT.Copy), p, t_os.get(pr - 2))
                    t_out[pr] = bav.free

            t_out = {}

            def out_turn(pr):
                for c in range(4):
                    p = q.pe(lambda e, c=c: e.transpose(bsel.t[:, 128 * c:128 * c + 128],
                                                        OS[:, pr % 2, 128 * c:128 * c + 128], identf[:, :]),
                             t_out[pr], bsel.free, t_idf)
                t_os[pr] = p

            def out_scale(pr):
                v = bsel.t[:, :].rearrange("p (c f k) -> p f c k", c=4, k=32)
                rc = small[:, pr % 2, 32:48].rearrange("p (c f) -> p f c", f=4)
                t_rc[pr] = q.dve(lambda e: e.reciprocal(rc, v[:, :, :, 8]), t_os[pr])

            t_rc = {}

            def out_write(pr, j):
                b, h, qh = pr // 8, 2 * (pr % 8) + j // 2, j % 2
                v = bsel.t[:, :].rearrange("p (c f k) -> p f c k", c=4, k=32)
                rc = small[:, pr % 2, 32:48].rearrange("p (c f) -> p f c", f=4)
                o = W[:, 8 * b + 4 * qh:8 * b + 4 * qh + 4, 8 * h:8 * h + 8]
                bsel.free = q.dve(lambda e: e.tensor_tensor(
                    o, v[:, j, :, 0:8], rc[:, j, :].unsqueeze(2).broadcast_to((128, 4, 8)), ALU.mult), t_rc[pr])

            LEAD = n2 + (14 if causal else 12)
            at = {}

            def plan(t, fn, *a):
                at.setdefault(t, []).append((fn, a))

            for u in range(UNITS):
                end = n * (u + 1) - 1
                plan(-1 if u < NS else LEAD + n2 * ((u - NS) // 2 + 1) + u % 2, fetch, u)
                plan(end + 2, max_end, u)
                plan(end + (7 if causal else 8), max_send, u)
            for pr in range(UNITS // 2):
                done = LEAD + n2 * (pr + 1) - 1 + 4
                plan(done + 2, out_turn, pr)
                plan(done + 3, out_scale, pr)
                for j in range(4):
                    plan(done + 4 + j, out_write, pr, j)
            total = n2 * (UNITS // 2)
            for T in range(-1, LEAD + total + 20):
                if 0 <= T < total:
                    max_step(T // n, T % n)
                g = T - LEAD
                if 0 <= g < total:
                    main_step(g // n2, g % n2)
                if g >= 7 and g % 4 == 3 and g // 4 - 1 < total // 4:
                    av_group(g // 4 - 1)
                for fn, a in at.get(T, ()):
                    fn(*a)
            q.barrier()
            for bkk in bank:
                bkk.free = None

        def project(wo, t_w, resid, dst, bias_row):
            toks = []
            for b in range(B):
                t = transposed(W, b, None, ZT)
                for c in (2 * b, 2 * b + 1):
                    bk = bank[c % 2]
                    for j in range(4):
                        k = 4 * c + j
                        p = q.pe(lambda e, bk=bk, j=j, k=k: e.matmul(bk.t[:, 128 * j:128 * j + 128],
                                                                     ZT[:, 128 * k:128 * k + 128], wo, start=True,
                                                                     stop=True), t, bk.free, t_w)
                    o = dst[:, 4 * c:4 * c + 4, :]
                    r = resid[:, 4 * c:4 * c + 4, :]
                    v = bk.t[:, :].rearrange("p (a b) -> p a b", a=4)
                    bk.free = q.dve(lambda e, o=o, r=r, v=v: e.tensor_tensor(o, r, v, ALU.add), p)
                    last = bk.free
                    if bias_row is not None:
                        last = q.dve(lambda e, o=o: e.tensor_tensor(o, o, bc[:, bias_row:bias_row + 1, :].broadcast_to(
                            (128, 4, 128)), ALU.add), bk.free, t_bc)
                toks.append(last)
            return toks

        def moe(nf, func, t_w, t_c, t_zt, t_ct, has_bias):
            cc = gs[:, 0, :].rearrange("p (t k) -> p t k", k=8)
            bh, by = bank[0:4], bank[4:6]
            hc = 0
            yc = 0
            t_y = {}
            hs = {}
            accs = {}

            def down(c, e, ht):
                nonlocal yc
                bk = by[yc % 2]
                yc += 1
                for j in range(4):
                    for f in range(nf):
                        k = (e % 2) * nf + f
                        p = q.pe(lambda en, bk=bk, j=j, f=f, k=k, e=e: en.matmul(
                            bk.t[:, 128 * j:128 * j + 128], PB[:, k, 128 * j:128 * j + 128],
                            W2[:, 128 * (e * nf + f):128 * (e * nf + f) + 128], start=(f == 0), stop=(f == nf - 1)),
                            ht, bk.free)
                t_y[(c, e)] = p
                for j in range(4):
                    t = 4 * c + j
                    o, v = W[:, t, :], bk.t[:, 128 * j:128 * j + 128]
                    s = cc[:, t, e:e + 1]
                    if (c, j) not in accs:
                        bk.free = q.dve(lambda en, o=o, v=v, s=s: en.tensor_scalar(o, v, s, None, ALU.mult), p, t_c)
                    else:
                        bk.free = q.dve(lambda en, o=o, v=v, s=s: en.scalar_tensor_tensor(
                            out=o, in0=v, scalar=s, in1=o, op0=ALU.mult, op1=ALU.add), p, accs[(c, j)], t_c)
                    accs[(c, j)] = bk.free

            prev = None
            order = [(c, e) for c in range(8) for e in range(8)]
            for idx, (c, e) in enumerate(order):
                if has_bias and e == 0:
                    bk = bank[6 + c % 2]
                    for j in range(4):
                        p = q.pe(lambda en, j=j, c=c, bk=bk: en.transpose(bk.t[0:8, 128 * j:128 * j + 128],
                                                                         cc[:, 4 * c + j, :], identf[:, :]), t_c, bk.free)
                    x = q.act(lambda en, c=c, bk=bk: en.activation(ctt[:, c % 2, :], bk.t[0:8, :], ACT.Copy), p)
                    for j in range(4):
                        p = q.pe(lambda en, j=j, c=c, bk=bk: en.matmul(bk.t[:, 128 * j:128 * j + 128],
                                                                       ctt[:, c % 2, 128 * j:128 * j + 128], b2s[:, :],
                                                                       start=True, stop=True), x, t_ct)
                    o = W[:, 4 * c:4 * c + 4, :].rearrange("p a b -> p (a b)")
                    bk.free = q.dve(lambda en, o=o, bk=bk: en.tensor_copy(o, bk.t[:, :]), p)
                    for j in range(4):
                        accs[(c, j)] = bk.free
                ht = []
                war = t_y.get(order[idx - 2]) if idx >= 2 else None
                for f in range(nf):
                    bk = bh[hc % 4]
                    hc += 1
                    p = q.pe(lambda en, bk=bk, f=f, e=e, c=c: en.matmul(
                        bk.t[:, :], W1[:, 128 * (e * nf + f):128 * (e * nf + f) + 128], ZT[:, 512 * c:512 * c + 512],
                        start=True, stop=True), bk.free, t_w, t_zt)
                    k = (e % 2) * nf + f
                    kw = dict(bias=cols[:, 8 + e * nf + f:9 + e * nf + f]) if has_bias else {}
                    bk.free = q.act(lambda en, bk=bk, k=k, kw=kw: en.activation(PB[:, k, :], bk.t[:, :], func, **kw), p,
                                    war, t_cols)
                    ht.append(bk.free)
                if prev is not None:
                    down(*prev)
                prev = (c, e, ht)
            down(*prev)
            return [accs[(c, 3)] for c in range(8)]

        def dv(fn, *w):
            return q.dve(fn, *w)

        gv = [gs[:, i, :] for i in range(14)]

        t_w0 = [load("w", WT[:, 0:640], ins["w_l0"])]
        t_m0 = [load("m", W1[:, 0:2048], ins["L0w1"]), load("m", W2[:, 0:2048], ins["L0w2"]), load("m", b2s[:, :], ins["L0b2"])]
        tz = []
        for b in range(B):
            r = ln_stats(X, b)
            z = ln_apply(Z, X, b, r)
            tz += transposed(Z, b, z, ZT)
        attention(0, WT[:, 0:128], WT[:, 128:256], WT[:, 256:384], cols[:, 4:5], cols[:, 5:6], bc[:, 1, :], None, t_w0, tz)
        ty = project(WT[:, 384:512], t_w0, Z, Z, 2)
        q.barrier()
        tz, t_yt = [], []
        for b in range(B):
            r = ln_stats(Z, b, ty[b])
            z = ln_apply(Z, Z, b, r)
            zs = Z[:, 8 * b:8 * b + 8, :]
            p1 = q.pool(lambda e, zs=zs: e.tensor_tensor(zs, zs, bc[:, 3:4, :].broadcast_to((128, 8, 128)), ALU.mult), z, t_bc)
            p2 = q.pool(lambda e, zs=zs: e.tensor_tensor(zs, zs, bc[:, 4:5, :].broadcast_to((128, 8, 128)), ALU.add), p1)
            t_yt.append(p2)
            tz += transposed(Z, b, p2, ZT)
        bk = bank[5]
        for t in range(NT):
            p = q.pe(lambda e, t=t: e.matmul(bk.t[:, 12 * t:12 * t + 12], ZT[:, 128 * t:128 * t + 128], WT[:, 512:524],
                                             start=True, stop=True), tz)
        gb = cols_gb = sb("gb", [128, 20])
        t_gb = load("gb", gb[:, :], ins["gate_b"].partition_broadcast(128))
        idx = sb("idx", [128, 8])
        t_idx = load("idx", idx[:, :], ins["idx"].partition_broadcast(128))
        lg = PB[:, 11, 0:384].rearrange("p (t k) -> p t k", k=12)
        a = dv(lambda e: e.tensor_tensor(lg[:, :, :], bk.t[:, 0:384].rearrange("p (t k) -> p t k", k=12),
                                         gb[:, 0:12].unsqueeze(1).broadcast_to((128, NT, 12)), ALU.add), p, t_gb)
        bk.free = a

        def v3(i, k):
            return gs[:, i, 0:NT * k].rearrange("p (t k) -> p t k", k=k)

        def first_max(lgv, mxi, k, w):
            m = gs[:, mxi + 1, 0:NT]
            a1 = dv(lambda e: e.tensor_reduce(m, lgv, AX.X, ALU.max), w)
            mb = m.unsqueeze(2).broadcast_to((128, NT, k))
            oh = v3(mxi, k)
            a2 = dv(lambda e: e.tensor_tensor(oh, lgv, mb, ALU.is_equal), a1)
            a3 = dv(lambda e: e.tensor_tensor(oh, oh, idx[:, 0:k].unsqueeze(1).broadcast_to((128, NT, k)), ALU.mult), a2, t_idx)
            c = gs[:, mxi + 2, 0:NT]
            a4 = dv(lambda e: e.tensor_reduce(c, oh, AX.X, ALU.max), a3)
            return dv(lambda e: e.tensor_tensor(oh, oh, c.unsqueeze(2).broadcast_to((128, NT, k)), ALU.is_equal), a4), a1

        lgv = lg[:, :, 0:4]
        t_oh, _ = first_max(lgv, 1, 4, a)
        gx = v3(4, 4)
        a = dv(lambda e: e.tensor_tensor(gx, lgv, gs[:, 2, 0:NT].unsqueeze(2).broadcast_to((128, NT, 4)), ALU.subtract), t_oh)
        a = q.act(lambda e: e.activation(gx, gx, ACT.Exp), a)
        gsum = gs[:, 5, 0:NT]
        a = dv(lambda e: e.tensor_reduce(gsum, gx, AX.X, ALU.add), a)
        l0 = lg[:, :, 4:8]
        l1 = lg[:, :, 8:12]
        em, x0, x1, f1, es = v3(6, 4), v3(7, 4), v3(8, 4), v3(9, 4), v3(10, 4)
        b1 = dv(lambda e: e.tensor_tensor(em, l0, l1, ALU.max), a)
        b2 = dv(lambda e: e.tensor_tensor(x0, l0, em, ALU.subtract), b1)
        b3 = dv(lambda e: e.tensor_tensor(x1, l1, em, ALU.subtract), b1)
        b4 = q.act(lambda e: e.activation(x0, x0, ACT.Exp), b2)
        b5 = q.act(lambda e: e.activation(x1, x1, ACT.Exp), b3)
        b6 = dv(lambda e: e.tensor_tensor(f1, l1, l0, ALU.is_gt), a)
        b7 = dv(lambda e: e.tensor_tensor(es, x0, x1, ALU.add), b4, b5)
        b8 = dv(lambda e: e.tensor_tensor(es, es, gsum.unsqueeze(2).broadcast_to((128, NT, 4)), ALU.mult), b7)
        b9 = dv(lambda e: e.reciprocal(es, es), b8)
        b10 = dv(lambda e: e.tensor_tensor(es, es, v3(1, 4), ALU.mult), b9)
        cc = gs[:, 0, :].rearrange("p (t g k) -> p t g k", g=4, k=2)
        b11 = dv(lambda e: e.tensor_tensor(cc[:, :, :, 1], es, f1, ALU.mult), b10, b6)
        b12 = dv(lambda e: e.tensor_tensor(cc[:, :, :, 0], es, cc[:, :, :, 1], ALU.subtract), b11)
        ta = moe(2, ACT.Relu, t_m0, b12, tz, t_m0, True)
        tr = []
        for b in range(B):
            zs = Z[:, 8 * b:8 * b + 8, :]
            ws = W[:, 8 * b:8 * b + 8, :]
            xs = X[:, 8 * b:8 * b + 8, :]
            a = dv(lambda e, zs=zs, ws=ws: e.tensor_tensor(zs, zs, ws, ALU.add), ta[2 * b:2 * b + 2])
            r = ln_stats(Z, b, a)
            z = ln_apply(Z, Z, b, r)
            p1 = q.pool(lambda e, zs=zs: e.tensor_tensor(zs, zs, bc[:, 5:6, :].broadcast_to((128, 8, 128)), ALU.mult), z)
            g2 = W[:, 8 * b:8 * b + 8, :]
            p2 = q.pool(lambda e, zs=zs, xs=xs: e.tensor_tensor(xs, xs, zs, ALU.add), p1)
            tr.append(p2)
        q.barrier()
        t_bc2 = load("bc2", bc[:, 0:1, :], ins["rows2"].partition_broadcast(128))
        for b in range(B):
            xs = X[:, 8 * b:8 * b + 8, :]
            tr[b] = q.pool(lambda e, xs=xs: e.tensor_tensor(xs, xs, bc[:, 0:1, :].broadcast_to((128, 8, 128)), ALU.add), t_bc2)

        t_wl = load("w", WT[:, 0:896], ins["w_l1"])
        t_rt = load("rt", W1[0:64, 0:2048], ins["rope"])
        bk = bank[0]
        p = q.pe(lambda e: e.matmul(bk.t[:, 0:320], WT[:, 0:128], WT[:, 128:448], start=True, stop=True), t_wl)
        WF = WT[:, 896:1216]
        f1_ = q.act(lambda e: e.activation(WF, bk.t[:, 0:320], ACT.Copy), p)
        rp0, rp1 = WT[:, 1216:1280], WT[:, 1280:1344]
        f2 = [q.dve(lambda e: e.tensor_copy(rp0[:, 0:32], WT[:, 576:608]), t_wl),
              q.dve(lambda e: e.tensor_copy(rp0[:, 32:64], WF[:, 256:288]), f1_),
              q.dve(lambda e: e.tensor_copy(rp1[:, 0:32], WT[:, 608:640]), t_wl),
              q.dve(lambda e: e.tensor_copy(rp1[:, 32:64], WF[:, 288:320]), f1_)]
        tz = []
        for b in range(B):
            r = ln_stats(X, b, tr[b])
            z = ln_apply(Z, X, b, r)
            tz += transposed(Z, b, z, ZT)
        OS2 = PB[:, 10, :]
        attention(1, WT[:, 448:576], WF[:, 0:128], WF[:, 128:256], cols[:, 6:7], cols[:, 6:7], None, (rp0, rp1),
                  [t_wl, f1_, f2, t_rt], tz)
        tx = project(WT[:, 640:768], t_wl, X, X, None)
        q.barrier()

        t_w3 = load("w", WT[:, 0:520], ins["w_l2"])
        t_m3 = [load("m", W1[:, :], ins["L1w1"]), load("m", W2[:, :], ins["L1w2"])]
        tz = []
        for b in range(B):
            r = ln_stats(X, b, tx[b])
            z = ln_apply(Z, X, b, r)
            r2 = ln_stats(Z, b, z)
            z2 = ln_apply(W, Z, b, r2)
            tz += transposed(W, b, z2, ZT, scale=cols[:, 24:25], bias=cols[:, 25:26])
        attention(2, WT[:, 0:128], WT[:, 128:256], WT[:, 256:384], cols[:, 6:7], cols[:, 6:7], None, None, t_w3, tz)
        ty = project(WT[:, 384:512], t_w3, Z, Z, None)
        q.barrier()
        tz = []
        for b in range(B):
            r = ln_stats(Z, b, ty[b])
            z = ln_apply(W, Z, b, r)
            tz += transposed(W, b, z, ZT, scale=cols[:, 26:27], bias=cols[:, 27:28])
            zs, xs = Z[:, 8 * b:8 * b + 8, :], X[:, 8 * b:8 * b + 8, :]
            tr[b] = q.pool(lambda e, zs=zs, xs=xs: e.tensor_tensor(xs, xs, zs, ALU.add), ty[b])
        bk = bank[5]
        for t in range(NT):
            p = q.pe(lambda e, t=t: e.matmul(bk.t[:, 8 * t:8 * t + 8], ZT[:, 128 * t:128 * t + 128], WT[:, 512:520],
                                             start=True, stop=True), tz)
        l8 = gs[:, 7, :].rearrange("p (t k) -> p t k", k=8)
        a = dv(lambda e: e.tensor_tensor(l8, bk.t[:, 0:256].rearrange("p (t k) -> p t k", k=8),
                                         gb[:, 12:20].unsqueeze(1).broadcast_to((128, NT, 8)), ALU.add), p)
        bk.free = a
        t_oh, _ = first_max(l8, 1, 8, a)
        a = dv(lambda e: e.tensor_copy(gs[:, 0, :], gs[:, 1, :]), t_oh)
        ta = moe(4, ACT.Gelu_apprx_tanh, t_m3, a, tz, None, False)
        od = out.rearrange("(t p) d -> p t d", p=128)
        outs = []
        for c in range(8):
            xs = X[:, 4 * c:4 * c + 4, :]
            a = dv(lambda e, xs=xs, c=c: e.tensor_tensor(xs, xs, W[:, 4 * c:4 * c + 4, :], ALU.add), ta[c], tr[c // 2])
            outs.append(q.dma("o", od[:, 4 * c:4 * c + 4, :], xs, a))
        q.finish([t for t in q.dma_open])
        block = ctx.enter_context(nc.Block())
        q.emit(block)


def kernel(**I):
    import numpy as _np
    import ml_dtypes
    import concourse.bacc as _bacc
    from concourse import mybir as _mybir
    from concourse.bass_utils import run_bass_kernel_spmd as _run

    f32 = _np.float32
    I = {k: _np.asarray(v) for k, v in I.items()}

    def chunks(a):
        n = a.shape[0] // 128
        return _np.concatenate([a[128 * c:128 * c + 128] for c in range(n)], axis=1)

    def rep4(a):
        z = _np.zeros((a.shape[0], 16), f32)
        return _np.concatenate([a, z] * 4, axis=1)

    def swap(a):
        return _np.concatenate([a[:, 16:32], a[:, 0:16]], axis=1)

    eye = _np.eye(128, dtype=f32)
    z1 = _np.zeros((128, 1), f32)
    cols = [I["L0_attn_norm_w"][:, None], I["L0_attn_norm_b"][:, None],
            I["L0_attn_b_in"][0:128, None], I["L0_attn_b_in"][128:256, None],
            I["L0_ffn_in_proj_b"][0:128, None], I["L0_ffn_in_proj_b"][128:256, None], z1, z1,
            I["L0_ffn_b1"].reshape(16, 128).T,
            I["L1_ffn_ln1_w"][:, None], I["L1_ffn_ln1_b"][:, None], I["L1_ffn_ln2_w"][:, None], I["L1_ffn_ln2_b"][:, None]]
    cols = _np.concatenate(cols, axis=1)
    cols = _np.concatenate([cols, _np.zeros((128, 40 - cols.shape[1]), f32)], axis=1)
    rows = _np.stack([I["L0_attn_b_out"], I["L0_ffn_in_proj_b"][256:384], I["L0_ffn_out_proj_b"],
                      I["L0_ffn_ln1_g"], I["L0_ffn_ln1_b"], I["L0_ffn_ln2_g"]])
    kk, qq = _np.meshgrid(_np.arange(128), _np.arange(128), indexing="ij")
    m_max = _np.where(qq > kk, NEG, 0.0)
    m_main = _np.where(kk > qq, NEG, 0.0)
    mask = _np.concatenate([m_max, m_main], axis=1).astype(ml_dtypes.bfloat16)
    w_ssm = _np.concatenate([chunks(I["L0_attn_W_in"]), chunks(rep4(I["L0_attn_A"])), chunks(rep4(I["L0_attn_B_ssm"])),
                             chunks(rep4(I["L0_attn_C_ssm"])), chunks(I["L0_attn_W_out"].T)], axis=1)
    w_l0 = _np.concatenate([I["L0_ffn_in_proj_w"].T, I["L0_ffn_out_proj_w"].T, I["L0_ffn_w_group"],
                            I["L0_ffn_w_expert"][:, :, 0].T, I["L0_ffn_w_expert"][:, :, 1].T,
                            _np.zeros((128, 116), f32)], axis=1)
    w_l1 = _np.concatenate([I["L1_attn_W_kv_down"].T, I["L1_attn_W_k_up"], I["L1_attn_W_v_up"], I["L1_attn_W_k_rope"],
                            swap(I["L1_attn_W_k_rope"]), I["L1_attn_W_q"], I["L1_attn_W_q_rope"],
                            swap(I["L1_attn_W_q_rope"]), I["L1_attn_W_o"], _np.zeros((128, 128), f32)], axis=1)
    w_l2 = _np.concatenate([I["L1_ffn_w_qkv"], I["L1_ffn_w_proj"], I["L1_ffn_gate_w"]], axis=1)
    inv = (f32(1.0) / _np.power(f32(10000.0), _np.arange(0, 32, 2, dtype=f32) / f32(32))).astype(f32)
    fr = _np.outer(_np.arange(S, dtype=f32), inv).astype(f32).T
    cs, sn = _np.cos(fr), _np.sin(fr)
    rope = _np.concatenate([_np.concatenate([cs, cs, cs, cs]), _np.concatenate([-sn, sn, -sn, sn])], axis=1).astype(f32)
    be = I["L0_ffn_b_expert"]
    arrays = {
        "x": I["L0_attn_x"].reshape(B * S, D), "cols": cols, "rows": rows, "rows2": I["L0_ffn_ln2_b"][None, :],
        "identf": eye, "identb": eye.astype(ml_dtypes.bfloat16), "maskb": mask,
        "ones": _np.ones((3, 1024), ml_dtypes.bfloat16), "zeros": _np.zeros((3, 1024), ml_dtypes.bfloat16),
        "idx": _np.arange(8, 0, -1).astype(f32),
        "gate_b": _np.concatenate([I["L0_ffn_b_group"], be[:, 0], be[:, 1], I["L1_ffn_gate_b"]]),
        "w_ssm": w_ssm, "w_l0": w_l0, "w_l1": w_l1, "w_l2": w_l2, "rope": rope,
        "L0w1": I["L0_ffn_w1"].transpose(1, 0, 2).reshape(128, 2048),
        "L0w2": I["L0_ffn_w2"].reshape(8, 2, 128, 128).transpose(2, 0, 1, 3).reshape(128, 2048),
        "L0b2": I["L0_ffn_b2"],
        "L1w1": I["L1_ffn_w1"].transpose(1, 0, 2).reshape(128, 4096),
        "L1w2": I["L1_ffn_w2"].reshape(8, 4, 128, 128).transpose(2, 0, 1, 3).reshape(128, 4096),
    }
    nc = _bacc.Bacc("TRN2", target_bir_lowering=False, num_devices=1)
    feed, aps = {}, {}
    for name, a in arrays.items():
        a = _np.ascontiguousarray(a)
        feed[f"in_{name}"] = a
        aps[name] = nc.dram_tensor(f"in_{name}", a.shape, _mybir.dt.from_np(a.dtype), kind="ExternalInput").ap()
    out = nc.dram_tensor("out_0", (B * S, D), F32, kind="ExternalOutput").ap()
    build(nc, aps, out)
    r = _run(nc, [feed], core_ids=[0])
    return r.results[0]["out_0"].reshape(B, S, D)
```

```python
from contextlib import ExitStack

import numpy as np
import concourse.bass as bass
from concourse import mybir

F32 = mybir.dt.float32
BF16 = mybir.dt.bfloat16
F32R = mybir.dt.float32r
ACT = mybir.ActivationFunctionType
ALU = mybir.AluOpType
AX = mybir.AxisListType

B, S, D = 4, 1024, 128
NT = 32
RATE0, RATE1 = (1, 1), (3, 1)
SIDE_STEPS, THEN_STEPS = 3, 5
AHEAD = 3
PIECES0, PIECES2 = 12, 11
H, HD = 16, 8
UNITS = B * H
EPS = 1e-5
NEG = -1.0e30


class Tok:

    def __init__(self, eng):
        self.eng, self.need, self.sem, self.val = eng, False, None, 0


class Queues:

    ENG = ("tensor", "scalar", "vector", "gpsimd", "sync")

    def __init__(self, nc, ctx):
        self.nc, self.ctx = nc, ctx
        self.q = {e: [] for e in self.ENG}
        self.last = {e: None for e in self.ENG}
        self.dma_n = {}
        self.dma_sems = {}
        self.dma_open = []

    def op(self, eng, fn, *waits):
        t = Tok(eng)
        self.q[eng].append((self.flat(waits), fn, t))
        self.last[eng] = t
        return t

    def pe(self, fn, *w):
        return self.op("tensor", fn, *w)

    def act(self, fn, *w):
        return self.op("scalar", fn, *w)

    def dve(self, fn, *w):
        return self.op("vector", fn, *w)

    def pool(self, fn, *w):
        return self.op("gpsimd", fn, *w)

    def flat(self, waits):
        out = []
        for w in waits:
            if isinstance(w, Tok):
                w.need = True
                out.append(w)
            elif w:
                out.extend(self.flat(w))
        return out

    def dma(self, stream, dst, src, *waits, eng="sync"):
        n = self.dma_n.get(stream, 0)
        self.dma_n[stream] = n + 1
        if stream not in self.dma_sems:
            self.dma_sems[stream] = self.ctx.enter_context(self.nc.semaphore("d_" + stream))
        t = Tok("dma")
        t.need, t.sem, t.val = True, self.dma_sems[stream], 16 * (n + 1)
        self.q[eng].append((self.flat(waits), lambda e: e.dma_start(dst, src), t))
        self.dma_open.append(t)
        return t

    def barrier(self, *extra):
        ends = [self.last[e] for e in ("tensor", "scalar", "vector", "gpsimd") if self.last[e] is not None]
        for e in self.ENG:
            self.q[e].append((self.flat([ends, extra]), None, None))
        return ends

    def finish(self, toks):
        self.q["sync"].append((self.flat([toks]), None, None))

    def emit(self, block):
        for e in ("tensor", "scalar", "vector", "gpsimd"):
            sem = self.ctx.enter_context(self.nc.semaphore("s_" + e))
            n = 0
            for _, _, t in self.q[e]:
                if t is not None and t.eng == e and t.need:
                    n += 1
                    t.sem, t.val = sem, n

        def program(name):
            def run(eng):
                seen = {}
                for waits, fn, t in self.q[name]:
                    best = {}
                    for w in waits:
                        if w.val > best.get(id(w.sem), (None, 0))[1]:
                            best[id(w.sem)] = (w.sem, w.val)
                    for k, (s, v) in best.items():
                        if seen.get(k, 0) < v:
                            eng.wait_ge(s, v)
                            seen[k] = v
                    if fn is None:
                        continue
                    ins = fn(eng)
                    if t.eng == "dma":
                        ins.then_inc(t.sem, 16)
                    elif t.need:
                        ins.then_inc(t.sem, 1)
            return run

        block.tensor(program("tensor"))
        block.scalar(program("scalar"))
        block.vector(program("vector"))
        block.gpsimd(program("gpsimd"))
        block.sync(program("sync"))


class Bank:

    def __init__(self, t):
        self.t, self.free, self.held = t, None, False


def build(nc, ins, out):
    with ExitStack() as ctx:
        q = Queues(nc, ctx)

        def sb(name, shape, dt=F32):
            return ctx.enter_context(nc.sbuf_tensor(name, shape, dt))

        X = sb("X", [128, NT, 128])
        Z = sb("Z", [128, NT, 128])
        W = sb("W", [128, NT, 128])
        VP = sb("VP", [128, NT, 168])
        PB = sb("PB", [128, 12, 512])
        NB = 4
        OS = sb("OS", [128, 2, 512])
        WT = sb("WT", [128, 1920])
        identf = sb("identf", [128, 128])
        identb = sb("identb", [128, 128], BF16)
        maskb = sb("maskb", [128, 256], BF16)
        bc = sb("bc", [128, 6, 128])
        cols = sb("cols", [128, 40])
        st = sb("st", [128, NT, 6])
        mv = sb("mv", [128, NT, 2])
        rs = sb("rs", [128, 4, NT])
        small = sb("small", [128, 4, 64])
        halves = sb("halves", [128, 8])
        nms = sb("nms", [24, 4, 128], BF16)
        gs = sb("gs", [128, 14, NT * 8])
        ctt = PB[0:8, 11, :]
        with ExitStack() as low:
            ZT, RK, W1, W2 = (low.enter_context(nc.sbuf_tensor(*a)) for a in (
                ("ZT", [128, NT * 128], F32), ("RK", [128, NB, 4, 1024], BF16), ("W1", [128, 4096], F32),
                ("W2", [128, 4096], F32)))
        y_low = sb("y_low", [128, NT * 128], F32R)
        w_high3 = sb("w_high3", [128, 4096], F32R)
        sb("gap_rk", [128, 2048])
        y_high = sb("y_high", [128, 2, 1024], F32R)
        w_low = sb("w_low", [128, 4096], F32R)
        sb("gap_w2", [128, 2048])
        w_high0 = sb("w_high0", [128, 2048], F32R)
        b2s = sb("b2s", [8, 128])
        bank = [Bank(ctx.enter_context(nc.psum_tensor(f"bank{i}", [128, 512], F32))) for i in range(8)]
        QD = nc.dram_tensor("q_parts", (B, 5, 128, 1024), BF16, kind="Internal").ap()
        KD = nc.dram_tensor("k_parts", (B, 5, 128, 1024), BF16, kind="Internal").ap()
        RQD = nc.dram_tensor("rq_parts", (B, 5, 32, 1024), BF16, kind="Internal").ap()
        RKD = nc.dram_tensor("rk_parts", (B, 5, 32, 1024), BF16, kind="Internal").ap()

        def load(stream, dst, src, *w, eng="sync"):
            return q.dma(stream, dst, src, *w, eng=eng)

        xin = ins["x"].rearrange("(t p) d -> p t d", p=128)
        tx = [q.dma("x%d" % b, X[:, 8 * b:8 * b + 8, :], xin[:, 8 * b:8 * b + 8, :]) for b in range(B)]
        t_cols = load("c_cols", cols[:, :], ins["cols"], eng="scalar")
        t_idf = load("c_idf", identf[:, :], ins["identf"], eng="scalar")
        t_idb = load("c_idb", identb[:, :], ins["identb"], eng="scalar")
        t_mask = load("c_mask", maskb[:, :], ins["maskb"], eng="scalar")
        t_bc = load("c_bc", bc[:, :, :], ins["rows"].partition_broadcast(128), eng="scalar")
        wssm = W2[:, 0:1280]
        t_ws = load("c_ws", wssm, ins["w_ssm"], eng="scalar")

        gb = sb("gb", [128, 20])
        idx = sb("idx", [128, 8])
        t_w0 = load("w0", WT[:, 0:524], ins["w_l0"])
        t_wl = load("wl", WT[:, 576:1472], ins["w_l1"])
        t_w1 = load("m", W1[:, 0:2048], ins["L0w1"])
        t_gb = load("gb", gb[:, :], ins["gate_b"].partition_broadcast(128))
        t_idx = load("idx", idx[:, :], ins["idx"].partition_broadcast(128))
        t_rt = load("rt", W1[0:64, 2048:4096], ins["rope"])
        t_vz = q.pool(lambda e: e.memset(VP[:, :, 144:168], 0.0))
        VH = VP[:, :, 0:144].rearrange("p t (h c) -> p t h c", c=9)
        t_vo = q.pool(lambda e: e.memset(VH[:, :, :, 8:9], 1.0))

        mn = [0]

        first_bank = [3]

        def misc(k=None):
            k = first_bank[0] if k is None else k
            for _ in range(3):
                mn[0] += 1
                if not bank[k + mn[0] % 3].held:
                    return bank[k + mn[0] % 3]
            raise RuntimeError("no bank")

        def run(g):
            for _ in g:
                pass

        def merge(first, needed, rate, *others):
            back.extend((g, rate) for g in others)
            n = 0
            for _ in first:
                n += 1
                if needed is not None and n % rate[0] == 0:
                    next(needed, None)
                for _ in range(rate[1]):
                    if back and next(back[0][0], back) is back:
                        back.pop(0)
            if needed is not None:
                run(needed)

        back = []

        def ln(src, b, dst, out, *w):
            lo, hi = 8 * b, 8 * b + 8
            k = lnk[0] % 2
            lnk[0] += 1
            a = []
            for t in range(lo, hi):
                a.append(q.dve(lambda e, t=t: e.bn_stats(st[:, t, :], src[:, t, :]), *w))
                if t % 4 == 3:
                    yield
            g = [q.dve(lambda e, t=t: e.bn_aggr(mv[:, t, :], st[:, t, :]), a[t - lo]) for t in range(lo, hi)]
            ve, r = rs[:, 0, lo:hi], rs[:, 2, lo:hi]
            t1 = q.pool(lambda e: e.tensor_scalar(ve, mv[:, lo:hi, 1], EPS, None, ALU.add), g[-1], q.last["gpsimd"])
            t_r = q.pool(lambda e: e.tensor_tensor(r, ve, halves[:, :], ALU.pow), t1, t_hv)
            yield
            yield
            for t in range(lo, hi):
                z = q.dve(lambda e, t=t: e.tensor_scalar(dst[:, t, :], src[:, t, :], mv[:, t, 0:1], rs[:, 2, t:t + 1],
                                                         ALU.subtract, ALU.mult), t_r)
            out.append(z)
            yield

        lnk = [0]

        def transposed(src, b, t_src, dst, scale=None, bias=None):
            toks = []
            for c in range(2 * b, 2 * b + 2):
                bk = misc()
                for j in range(4):
                    p = q.pe(lambda e, j=j, c=c, bk=bk: e.transpose(bk.t[:, 128 * j:128 * j + 128], src[:, 4 * c + j, :],
                                                                    identf[:, :]), t_src, bk.free, t_idf)
                o = dst[:, 512 * c:512 * c + 512]
                if scale is None:
                    bk.free = q.act(lambda e, o=o, bk=bk: e.activation(o, bk.t[:, :], ACT.Copy), p)
                else:
                    bk.free = q.act(lambda e, o=o, bk=bk: e.activation(o, bk.t[:, :], ACT.Identity, bias=bias,
                                                                       scale=scale), p, t_cols)
                toks.append(bk.free)
            return toks

        t_hv = q.pool(lambda e: e.memset(halves[:, :], -0.5))

        def chained(gens):
            gens = list(gens)
            live = []
            while gens or live:
                if gens:
                    live.append(gens.pop(0))
                for _ in range(AHEAD):
                    for g in list(live):
                        if next(g, live) is live:
                            live.remove(g)
                        yield

        def chain(gens):
            run(chained(gens))

        t_ssm_in = []

        def ssm_in(b):
            z, z2 = [], []
            yield from ln(X, b, Z, z, tx[b])
            yield from ln(Z, b, W, z2, z)
            yield
            t_ssm_in.extend(transposed(W, b, z2, ZT, scale=cols[:, 0:1], bias=cols[:, 1:2]))

        chain(ssm_in(b) for b in range(B))
        w_in = wssm[:, 0:256].rearrange("p (c n) -> p c n", c=2)
        a_rep = wssm[:, 256:512].rearrange("p (c n) -> p c n", c=2)
        b_rep = wssm[:, 512:768].rearrange("p (c n) -> p c n", c=2)
        c_rep = wssm[:, 768:1024].rearrange("p (c n) -> p c n", c=2)
        wo_t = wssm[:, 1024:1280].rearrange("p (c n) -> p c n", c=2)
        gsb = W2[:, 1280:1344]
        h4 = W2[:, 1344:1472]
        bb = cols[:, 36:40]
        bk0 = bank[0]
        for c in range(2):
            q.pe(lambda e, c=c: e.matmul(bk0.t[:, 0:32], w_in[:, c, :], a_rep[:, c, 0:32], start=(c == 0), stop=(c == 1)), t_ws)
        for c in range(2):
            p = q.pe(lambda e, c=c: e.matmul(bk0.t[:, 32:64], w_in[:, c, :], b_rep[:, c, 0:32], start=(c == 0), stop=(c == 1)))
        t_g = q.act(lambda e: e.activation(gsb, bk0.t[:, 0:64], ACT.Copy), p)
        bk1 = bank[1]
        for c in range(2):
            p = q.pe(lambda e, c=c: e.matmul(bk1.t[:, 0:128], c_rep[:, c, :], wo_t[:, c, :], start=(c == 0), stop=(c == 1)))
        t_h = q.act(lambda e: e.activation(h4, bk1.t[:, 0:128], ACT.Copy), p)
        bk2 = bank[2]
        for i, rep in enumerate((a_rep, b_rep)):
            for c in range(2):
                p = q.pe(lambda e, c=c, i=i, rep=rep: e.matmul(bk2.t[:, i:i + 1], rep[:, c, :], cols[:, 2 + c:3 + c],
                                                               start=(c == 0), stop=(c == 1)), t_cols)
        t_b1 = q.dve(lambda e: e.tensor_scalar(bb[:, 0:1], bk2.t[:, 0:1], -1.0, None, ALU.mult), p)
        t_b2 = q.dve(lambda e: e.tensor_copy(bb[:, 1:2], bk2.t[:, 1:2]), p)
        q.barrier()
        A_s, U_s, S_s = PB[:, 0:2, :], PB[:, 2:4, :], PB[:, 4:6, :]
        pa = []
        for i, base in ((0, 2), (1, 4)):
            for hf in range(2):
                for b in range(B):
                    p = q.pe(lambda e, i=i, base=base, hf=hf, b=b: e.matmul(
                        bank[base + hf].t[32 * b:32 * b + 32, :], gsb[:, 32 * i:32 * i + 32],
                        ZT[:, 1024 * b + 512 * hf:1024 * b + 512 * hf + 512], start=True, stop=True), t_g)
                pa.append(p)
        ta = []
        for hf in range(2):
            x = q.act(lambda e, hf=hf: e.activation(A_s[:, hf, :], bank[2 + hf].t[:, :], ACT.Exp, bias=bb[:, 0:1],
                                                    scale=-1.0), pa[hf], t_b1)
            bank[2 + hf].free = x
            y = q.dve(lambda e, hf=hf: e.tensor_scalar(A_s[:, hf, :], A_s[:, hf, :], 1.0, None, ALU.add), x)
            ta.append(q.dve(lambda e, hf=hf: e.reciprocal(A_s[:, hf, :], A_s[:, hf, :]), y))
            tu = q.act(lambda e, hf=hf: e.activation(U_s[:, hf, :], bank[4 + hf].t[:, :], ACT.Identity, bias=bb[:, 1:2]),
                       pa[2 + hf], t_b2)
            bank[4 + hf].free = tu
            ta.append(tu)
        t_scan = q.dve(lambda e: e.tensor_tensor_scan(S_s.rearrange("p a b -> p (a b)"), A_s.rearrange("p a b -> p (a b)"),
                                                      U_s.rearrange("p a b -> p (a b)"), 0.0, ALU.mult, ALU.add), ta)
        t_x, ssm_bias = [], []
        for b in range(B):
            zs = Z[:, 8 * b:8 * b + 8, :]
            p1 = q.pool(lambda e, zs=zs: e.tensor_tensor(zs, zs, bc[:, 0:1, :].broadcast_to((128, 8, 128)), ALU.add), t_bc)
            xs = X[:, 8 * b:8 * b + 8, :]
            t_x.append(q.pool(lambda e, xs=xs, zs=zs: e.tensor_tensor(xs, xs, zs, ALU.add), p1))
            ssm_bias.append(p1)
        sv = S_s.rearrange("p a b -> p (a b)")
        ssm_done = []

        def ssm_out(b):
            for c in (2 * b, 2 * b + 1):
                bk = bank[c % 2]
                for j in range(4):
                    tt = (4 * c + j) % 8
                    p = q.pe(lambda e, bk=bk, j=j, tt=tt: e.matmul(
                        bk.t[:, 128 * j:128 * j + 128], sv[32 * b:32 * b + 32, 128 * tt:128 * tt + 128],
                        h4[32 * b:32 * b + 32, :], start=True, stop=True), t_scan, t_h, bk.free)
                xs = X[:, 4 * c:4 * c + 4, :].rearrange("p a b -> p (a b)")
                bk.free = q.dve(lambda e, xs=xs, bk=bk: e.tensor_tensor(xs, xs, bk.t[:, :], ALU.add), p, t_x[b])
            t_x[b] = bk.free
            ssm_done.append(p)

        for b in range(B):
            ssm_out(b)
        ended = [[ssm_done[-1]]]

        lo3 = OS[:, :, :].rearrange("p a b -> p (a b)").bitcast(BF16)[:, 0:1024].rearrange("p (s n) -> p s n", s=2)

        outs_done = {}
        preps = {}

        class Prep:

            def __init__(self, layer, wq, wk, wv, qb, kb, vb, wrope, t_w):
                self.causal, self.layer, self.queued = layer == 1, layer, set()
                self.busy = set()
                self.wq, self.wk, self.wv, self.qb, self.kb, self.vb, self.wrope, self.t_w = wq, wk, wv, qb, kb, vb, wrope, t_w
                self.wr, self.slot_done, self.n, self.t_v = {}, [ended[-1], ended[-1]], 0, None
                if self.causal:
                    self.q_seq, self.k_seq = ((0, 2), (1, 3), (4,)), ((2, 3), (1, 4), (0,))
                else:
                    self.q_seq, self.k_seq = ((0, 3), (1, 4), (2,)), ((0,), (1,), (2,))

            def scratch(self, b, s, rows):
                if self.layer == 2:
                    lo = W1[0:rows, 2048 + 256 * s:2304 + 256 * s].bitcast(BF16)
                elif self.layer == 1 and b == B - 1:
                    lo = gs[0:rows, 2 + s, :].bitcast(BF16)
                else:
                    return (PB[0:rows, 4 + 2 * s, :], PB[0:rows, 5 + 2 * s, :].bitcast(BF16), lo3[0:rows, s, :],
                            PB[0:64, 8, :])
                return (W1[0:rows, 1024 * s:1024 * s + 512], W1[0:rows, 1024 * s + 512:1024 * s + 1024].bitcast(BF16), lo,
                        gs[0:64, 4:6, :].rearrange("p a b -> p (a b)"))

            def parts(self, bkk, p, rows, bias, dst, c, extra=None):
                if extra is None:
                    bkk.held = True
                    yield
                while self.busy == {0, 1}:
                    yield
                s = self.n % 2 if self.n % 2 not in self.busy else 1 - self.n % 2
                self.n = s + 1
                self.busy.add(s)
                prev = self.slot_done[s]
                x, sp, lo, _ = self.scratch(c // 2, s, rows)
                r1 = x
                hi, mid = sp[:, 0:512], sp[:, 512:1024]
                if extra is None:
                    x1 = q.act(lambda e: e.activation(x, bkk.t[0:rows, :], ACT.Identity, bias=bias), p, prev, t_cols)
                    h1 = q.act(lambda e: e.activation(hi, bkk.t[0:rows, :], ACT.Identity, bias=bias), p)
                    bkk.free, bkk.held = h1, False
                else:
                    x1 = extra(x, prev)
                    h1 = q.act(lambda e: e.activation(hi, x, ACT.Copy), x1, prev)
                yield
                d1 = q.dve(lambda e: e.tensor_tensor(r1, x, hi, ALU.subtract), h1, x1)
                d2 = q.dve(lambda e: e.tensor_copy(mid, r1), d1)
                d3 = q.dve(lambda e: e.tensor_tensor(lo, r1, mid, ALU.subtract), d2)
                b, tc = c // 2, slice(512 * (c % 2), 512 * (c % 2) + 512)
                ds = []
                for k, src in enumerate((hi, mid, lo)):
                    for dd, r0, nr, seq in dst:
                        for m in seq[k]:
                            ds.append(q.dma("sc%d" % s, dd[b, m, :, tc], src[r0:r0 + nr, :], d3))
                self.slot_done[s] = ds
                self.busy.remove(s)
                self.wr.setdefault(b, []).extend(ds)

            def qkv(self, b, t_zt):
                for c in (2 * b, 2 * b + 1):
                    zc = ZT[:, 512 * c:512 * c + 512]
                    for wt, bias, dst in ((self.wq, self.qb, [(QD, 0, 128, self.q_seq)]),
                                          (self.wk, self.kb, [(KD, 0, 128, self.k_seq)])):
                        bkk = misc()
                        p = q.pe(lambda e, bkk=bkk, wt=wt, zc=zc: e.matmul(bkk.t[:, :], wt, zc, start=True, stop=True),
                                 bkk.free, self.t_w, t_zt)
                        yield from self.parts(bkk, p, 128, bias, dst, c)
                        yield
                    if self.causal:
                        b0, b1 = misc(), misc()
                        p0 = q.pe(lambda e, b0=b0, zc=zc: e.matmul(b0.t[0:64, :], self.wrope[0], zc, start=True,
                                                                   stop=True), b0.free)
                        p1 = q.pe(lambda e, b1=b1, zc=zc: e.matmul(b1.t[0:64, :], self.wrope[1], zc, start=True,
                                                                   stop=True), b1.free)

                        b0.held = b1.held = True

                        def rot(x, prev, c=c, p0=p0, p1=p1, b0=b0, b1=b1):
                            o = 2048 + 512 * (c % 2)
                            m0 = q.dve(lambda e: e.tensor_tensor(x, b0.t[0:64, :], W1[0:64, o:o + 512], ALU.mult), p0,
                                       prev, self.t_w)
                            y = self.scratch(c // 2, 0, 64)[3]
                            m1 = q.dve(lambda e: e.tensor_tensor(y, b1.t[0:64, :], W1[0:64, 1024 + o:1536 + o], ALU.mult),
                                       p1)
                            b0.free, b1.free, b0.held, b1.held = m0, m1, False, False
                            return q.dve(lambda e: e.tensor_tensor(x, x, y, ALU.add), m1)
                        yield from self.parts(b0, p0, 64, None, [(RQD, 0, 32, self.q_seq), (RKD, 32, 32, self.k_seq)], c, rot)
                        yield
                    bkk = misc()
                    for j in range(4):
                        p = q.pe(lambda e, bkk=bkk, c=c, j=j: e.matmul(bkk.t[:, 128 * j:128 * j + 128],
                                                                       ZT[:, 512 * c + 128 * j:512 * c + 128 * j + 128],
                                                                       self.wv, start=True, stop=True), bkk.free)
                    bkk.held = True
                    yield
                    bkk.held = False
                    i0 = bkk.t[:, :].rearrange("p (t h c) -> p t h c", t=4, c=8)
                    vb = self.vb
                    for j in range(4):
                        o = VH[:, 4 * c + j, :, 0:8]
                        if vb is None:
                            bkk.free = q.act(lambda e, o=o, i0=i0, j=j: e.activation(o, i0[:, j], ACT.Copy), p, t_vz, t_vo)
                        else:
                            bkk.free = q.dve(lambda e, o=o, i0=i0, j=j: e.tensor_tensor(
                                o, i0[:, j], vb.rearrange("p (h c) -> p h c", c=8), ALU.add), p, t_bc, t_vz, t_vo)
                    self.t_v = bkk.free
                    if c % 2:
                        self.queued.add(b)
                    yield

        class Rings:

            def __init__(self, prep):
                self.prep, self.loaded, self.mained = prep, {}, {}
                self.NS = 6 if prep.causal else 8
                self.t_fill, self.late = {}, []

            def slot(self, u, k, r0=0, r1=128):
                s = u % self.NS
                if not self.prep.causal:
                    return RK[r0:r1, s // 2, 2 * (s % 2) + k, :]
                if s < 4:
                    return RK[r0:r1, s, k, :]
                return W2[r0:r1, 2048 * (s - 4) + 512 * k:2048 * (s - 4) + 512 * k + 512].bitcast(BF16)

            def fill(self, slots, used):
                for s in slots:
                    if self.prep.causal:
                        src = ins["fill"][24:32, 0:4096]
                        if s < 4:
                            z = q.dma("z%d" % s, RK[M0:E0, s, :, :], src.rearrange("p (b c) -> p b c", b=4), used)
                        else:
                            z = q.dma("z%d" % s, W2[M0:E0, 2048 * (s - 4):2048 * (s - 3)].bitcast(BF16), src, used)
                    elif s % 2 == 0:
                        z = q.dma("z%d" % (s // 2), RK[72:128, s // 2, :, :],
                                  ins["fill"][:, 0:4096].rearrange("p (b c) -> p b c", b=4), used)
                    self.t_fill[s] = z

            def fetch(self, u):
                s, b, h = u % self.NS, u // H, u % H
                r = slice(8 * h, 8 * h + 8)
                assert b in self.prep.queued
                w = [self.t_fill[s], self.prep.wr[b], self.mained.get(u - self.NS)]
                L = []

                def cp(k, row, src):
                    L.append(q.dma("ld%d" % s, self.slot(u, k, row, row + src.shape[0] * src.shape[1]), src, w))
                if self.prep.causal:
                    cp(0, E0, QD[b, 0:3, r, :])
                    cp(1, E0, KD[b, 2:5, r, :])
                    cp(2, E0, QD[b, 2:5, r, :])
                    cp(3, E0, KD[b, 0:3, r, :])
                    if h < self.NS:
                        cp(0, 0, RQD[b, 0:3])
                        cp(1, 0, RKD[b, 2:5])
                        cp(2, 0, RQD[b, 2:5])
                        cp(3, 0, RKD[b, 0:3])
                else:
                    for i in range(3):
                        cp(0, 24 * i, QD[b, i:i + 3, r, :])
                        cp(1, 24 * i, KD[b, 0:3, r, :])
                if u >= self.NS:
                    L.append(q.pool(lambda e: e.memset(self.slot(u, 0, M0, M0 + 3), 0.0), self.mained[u - self.NS],
                                    q.last["gpsimd"]))
                self.loaded[u] = L

            def first(self, slots):
                for u in slots:
                    self.fetch(u)

        M0 = 96
        E0 = 104

        def attention(rings, side, then, pieces, spread=None, start=None, hooks=()):
            prep = rings.prep
            causal = prep.causal
            scale = 1.0 / float(np.sqrt(40.0 if causal else 8.0))
            NS, slot, loaded, mained = rings.NS, rings.slot, rings.loaded, rings.mained

            if causal:
                mains = [(kt, hh, qh, max(0, 128 * kt - 512 * qh)) for kt in range(8) for hh in range(2)
                         for qh in range(kt // 4, 2)]
                maxes = [(qt, kh, min(512, 128 * (qt + 1) - 512 * kh)) for qt in range(8) for kh in range(qt // 4 + 1)]
                t_m2 = q.pool(lambda e: e.memset(small[:, 0:2, 0:16], NEG), q.last["vector"])
            else:
                mains = [(kt, hh, qh, 0) for kt in range(8) for hh in range(2) for qh in range(2)]
                maxes = [(qt, kh, 512) for qt in range(8) for kh in range(2)]
                t_m2 = None
            n, n2 = len(maxes), len(mains)
            assert n2 == 2 * n
            bmain, bav, bsel = bank[0:3], bank[6], bank[7]
            t_nm, sent, t_exp, t_av, t_os, maxed = {}, {}, {}, {}, {}, {}
            NPB = 12

            def max_step(u, i):
                qt, kh, wd = maxes[i]
                bkk = misc(3)
                diag = causal and kh == qt // 4
                w = loaded[u] if i == 0 else None
                p = q.pe(lambda e: e.matmul(bkk.t[:, 0:wd], slot(u, 0)[:, 128 * qt:128 * qt + 128],
                                            slot(u, 1)[:, 512 * kh:512 * kh + wd], start=True, stop=not diag), bkk.free, w)
                if diag:
                    p = q.pe(lambda e: e.matmul(bkk.t[:, wd - 128:wd], identb[:, :], maskb[:, 0:128], start=False,
                                                stop=True), t_idb, t_mask)
                m2 = small[:, u % 2, 0:16]
                bkk.free = q.dve(lambda e: e.tensor_reduce(m2[:, 2 * qt + kh:2 * qt + kh + 1], bkk.t[:, 0:wd], AX.X,
                                                           ALU.max), p, t_m2)
                if i == n - 1:
                    maxed[u] = bkk.free

            def max_end(u):
                k = u % 2
                m2, nm, r1 = small[:, k, 0:16], small[:, k, 16:24], small[:, k, 24:32]
                pts = small[:, 2 + k, 0:32].bitcast(BF16)
                a = q.dve(lambda e: e.tensor_reduce(nm, m2.rearrange("p (a b) -> p a b", b=2), AX.X, ALU.max, negate=True),
                          maxed[u])
                b_ = q.pool(lambda e: e.tensor_copy(pts[:, 0:8], nm), a, q.last["gpsimd"])
                c = q.pool(lambda e: e.tensor_tensor(r1, nm, pts[:, 0:8], ALU.subtract), b_)
                d = q.pool(lambda e: e.tensor_copy(pts[:, 8:16], r1), c)
                t_nm[u] = q.pool(lambda e: e.tensor_tensor(pts[:, 16:24], r1, pts[:, 8:16], ALU.subtract), d)

            def max_send(u):
                pts = small[:, 2 + u % 2, 0:32].bitcast(BF16)
                tb = bsel.t[0:24, 0:64].bitcast(BF16)
                p = q.pe(lambda e: e.transpose(tb, pts[:, 0:24], identb[:, :]), t_nm[u], bsel.free, t_idb)
                o = nms[:, u % 4, :]
                bsel.free = q.act(lambda e: e.activation(o, tb, ACT.Copy), p, sent.get(u - 4))
                sent[u] = q.dma("nm%d" % (u % 4), slot(u, 0, M0, M0 + 3).rearrange("p (t c) -> p t c", t=8), o,
                                bsel.free, loaded[u], maxed[u])

            def main_step(pr, i):
                kt, hh, qh, c0 = mains[i]
                u = 2 * pr + hh
                g = pr * n2 + i
                bkk = bmain[g % 3]
                w = sent[u] if kt == 0 else None
                qs = slice(512 * qh + c0, 512 * qh + 512)
                ks = slice(128 * kt, 128 * kt + 128)
                diag = causal and kt // 4 == qh
                p = q.pe(lambda e: e.matmul(bkk.t[:, c0:512], slot(u, 1)[:, ks], slot(u, 0)[:, qs], start=True,
                                            stop=not causal), bkk.free, w)
                if causal:
                    p = q.pe(lambda e: e.matmul(bkk.t[:, c0:512], slot(u, 3)[:, ks], slot(u, 2)[:, qs], start=False,
                                                stop=not diag))
                if diag:
                    p = q.pe(lambda e: e.matmul(bkk.t[:, c0:c0 + 128], identb[:, :], maskb[:, 128:256], start=False,
                                                stop=True))
                mained[u] = p
                o = PB[:, g % NPB, c0:512]
                bkk.free = q.act(lambda e: e.activation(o, bkk.t[:, c0:512], ACT.Exp, scale=scale), p,
                                 t_av.get(g - NPB), prep.slot_done)
                t_exp[g] = bkk.free

            def av_group(gg):
                for g in range(4 * gg, 4 * gg + 4):
                    pr, i = g // n2, g % n2
                    kt, hh, qh, c0 = mains[i]
                    b, h = pr // 8, 2 * (pr % 8) + hh
                    j = 2 * hh + qh
                    p = q.pe(lambda e, g=g, b=b, h=h, kt=kt, c0=c0, j=j, qh=qh: e.matmul(
                        bav.t[32 * j:32 * j + 32, c0:512], VP[:, 8 * b + kt, 9 * h:9 * h + 32], PB[:, g % NPB, c0:512],
                        start=(kt == 0), stop=(kt == (3 + 4 * qh if causal else 7))), t_exp[g], bav.free, prep.t_v, t_vz, t_vo)
                    t_av[g] = p
                if (gg + 1) % (n2 // 4) == 0:
                    pr = (gg + 1) // (n2 // 4) - 1
                    o = OS[:, pr % 2, :]
                    bav.free = q.act(lambda e: e.activation(o, bav.t[:, :], ACT.Copy), p, t_os.get(pr - 2))
                    t_out[pr] = bav.free

            t_out = {}

            def out_turn(pr):
                for c in range(4):
                    p = q.pe(lambda e, c=c: e.transpose(bsel.t[:, 128 * c:128 * c + 128],
                                                        OS[:, pr % 2, 128 * c:128 * c + 128], identf[:, :]),
                             t_out[pr], bsel.free, t_idf)
                t_os[pr] = p

            def out_scale(pr):
                v = bsel.t[:, :].rearrange("p (c f k) -> p f c k", c=4, k=32)
                rc = small[:, pr % 2, 32:48].rearrange("p (c f) -> p f c", f=4)
                t_rc[pr] = q.dve(lambda e: e.reciprocal(rc, v[:, :, :, 8]), t_os[pr])

            t_rc = {}

            def out_write(pr, j):
                b, h, qh = pr // 8, 2 * (pr % 8) + j // 2, j % 2
                v = bsel.t[:, :].rearrange("p (c f k) -> p f c k", c=4, k=32)
                rc = small[:, pr % 2, 32:48].rearrange("p (c f) -> p f c", f=4)
                o = W[:, 8 * b + 4 * qh:8 * b + 4 * qh + 4, 8 * h:8 * h + 8]
                bsel.free = q.dve(lambda e: e.tensor_tensor(
                    o, v[:, j, :, 0:8], rc[:, j, :].unsqueeze(2).broadcast_to((128, 4, 8)), ALU.mult), t_rc[pr])
                outs_done[b] = bsel.free

            LEAD = n2 + (14 if causal else 12)
            at = {}

            def plan(t, fn, *a):
                at.setdefault(t, []).append((fn, a))

            for u in range(UNITS):
                end = n * (u + 1) - 1
                if u >= NS:
                    plan(LEAD + n2 * ((u - NS) // 2 + 1) + u % 2, rings.fetch, u)
                plan(end + 2, max_end, u)
                plan(end + (7 if causal else 8), max_send, u)
            for pr in range(UNITS // 2):
                done = LEAD + n2 * (pr + 1) - 1 + 4
                plan(done + 2, out_turn, pr)
                plan(done + 3, out_scale, pr)
                for j in range(4):
                    plan(done + 4 + j, out_write, pr, j)
            total = n2 * (UNITS // 2)
            for T in range(-1, LEAD + total + 20):
                first_bank[0] = 0 if T < LEAD else 3
                if T >= 0 and T < LEAD:
                    next(side, None)
                if T == LEAD - 1:
                    run(side)
                if spread is not None and T >= 0 and (T < LEAD or T % SIDE_STEPS == 0):
                    next(spread, None)
                if T == LEAD - 1:
                    while any(bank[k].held for k in range(3)):
                        next(spread)
                if T == 8:
                    rings.first(rings.late)
                if start is None and pieces and T > total and T % 5 == 0:
                    next(then)
                    pieces -= 1
                if start is not None and T % THEN_STEPS == 0:
                    for t0, g in zip(start, then):
                        if T >= t0 and next(g, start) is not start:
                            break
                for t0, fn in hooks:
                    if T == t0:
                        fn()
                if 0 <= T < total:
                    max_step(T // n, T % n)
                g = T - LEAD
                if 0 <= g < total:
                    main_step(g // n2, g % n2)
                if g >= 7 and g % 4 == 3 and g // 4 - 1 < total // 4:
                    av_group(g // 4 - 1)
                for fn, a in at.get(T, ()):
                    fn(*a)
            ended.append([t_av[total - 1], t_os[UNITS // 2 - 1]])

        def project(b, wo, t_w, resid, dst, bias_row):
            t = transposed(W, b, outs_done[b], ZT)
            yield
            for c in (2 * b, 2 * b + 1):
                bk = misc()
                for j in range(4):
                    k = 4 * c + j
                    p = q.pe(lambda e, bk=bk, j=j, k=k: e.matmul(bk.t[:, 128 * j:128 * j + 128],
                                                                 ZT[:, 128 * k:128 * k + 128], wo, start=True,
                                                                 stop=True), t, bk.free, t_w)
                bk.held = True
                yield
                bk.held = False
                o = dst[:, 4 * c:4 * c + 4, :]
                r = resid[:, 4 * c:4 * c + 4, :]
                v = bk.t[:, :].rearrange("p (a b) -> p a b", a=4)
                bk.free = q.dve(lambda e, o=o, r=r, v=v: e.tensor_tensor(o, r, v, ALU.add), p)
                last = bk.free
                if bias_row is not None:
                    last = q.dve(lambda e, o=o: e.tensor_tensor(o, o, bc[:, bias_row:bias_row + 1, :].broadcast_to(
                        (128, 4, 128)), ALU.add), bk.free, t_bc)
                yield
            proj[b] = last

        proj = {}
        ccv = gs[:, 0, :].rearrange("p (t k) -> p t k", k=8)
        mo = {"h": 0, "y": 0, "prev": None, "t_y": []}
        accs = {}

        def down(c, e, ht, nf, t_c):
            bk = bank[6 + mo["y"] % 2]
            mo["y"] += 1
            for j in range(4):
                for f in range(nf):
                    k = (e % 2) * nf + f
                    p = q.pe(lambda en, bk=bk, j=j, f=f, k=k, e=e: en.matmul(
                        bk.t[:, 128 * j:128 * j + 128], PB[:, k, 128 * j:128 * j + 128],
                        W2[:, 128 * (e * nf + f):128 * (e * nf + f) + 128], start=(f == 0), stop=(f == nf - 1)),
                        ht, bk.free)
            mo["t_y"].append(p)
            for j in range(4):
                t = 4 * c + j
                o, v = W[:, t, :], bk.t[:, 128 * j:128 * j + 128]
                s = ccv[:, t, e:e + 1]
                if (c, j) not in accs:
                    bk.free = q.dve(lambda en, o=o, v=v, s=s: en.tensor_scalar(o, v, s, None, ALU.mult), p, t_c)
                else:
                    bk.free = q.dve(lambda en, o=o, v=v, s=s: en.scalar_tensor_tensor(
                        out=o, in0=v, scalar=s, in1=o, op0=ALU.mult, op1=ALU.add), p, accs[(c, j)], t_c)
                accs[(c, j)] = bk.free

        def split_w(n, hi, engine_l, *w):
            t = []
            for i in range(n // 512):
                c = slice(512 * i, 512 * i + 512)
                h = q.act(lambda e, c=c: e.activation(hi[:, c], W1[:, c], ACT.Copy), *w)
                t.append(engine_l(lambda e, c=c: e.tensor_tensor(w_low[:, c], W1[:, c], hi[:, c].bitcast(F32),
                                                                 ALU.subtract), h))
            return t

        def split_y(b, t_lg):
            t = []
            for i in range(2):
                c = slice(1024 * b + 512 * i, 1024 * b + 512 * i + 512)
                z, zl, o = ZT[:, c], y_low[:, c], y_high[:, b % 2, 512 * i:512 * i + 512]
                h = q.act(lambda e, z=z, o=o: e.activation(o, z, ACT.Copy), t_yt[b], ended[-1])
                t.append(q.dve(lambda e, z=z, zl=zl, o=o: e.tensor_tensor(zl, z, o.bitcast(F32), ALU.subtract), h, t_lg))
            return t

        def moe(b, nf, func, w_hi, t_w, t_c, t_zt, has_bias):
            for c in (2 * b, 2 * b + 1):
                for j in range(4):
                    accs.pop((c, j), None)
                for e in range(8):
                    if has_bias and e == 0:
                        bk = misc()
                        for j in range(4):
                            p = q.pe(lambda en, j=j, c=c, bk=bk: en.transpose(bk.t[0:8, 128 * j:128 * j + 128],
                                                                             ccv[:, 4 * c + j, :], identf[:, :]), t_c, bk.free)
                        x = q.act(lambda en, c=c, bk=bk: en.activation(ctt, bk.t[0:8, :], ACT.Copy), p)
                        bk.free = x
                        bk = misc()
                        for j in range(4):
                            p = q.pe(lambda en, j=j, c=c, bk=bk: en.matmul(bk.t[:, 128 * j:128 * j + 128],
                                                                           ctt[:, 128 * j:128 * j + 128], b2s[:, :],
                                                                           start=True, stop=True), x, t_w, bk.free)
                        o = W[:, 4 * c:4 * c + 4, :].rearrange("p a b -> p (a b)")
                        bk.free = q.dve(lambda en, o=o, bk=bk: en.tensor_copy(o, bk.t[:, :]), p)
                        for j in range(4):
                            accs[(c, j)] = bk.free
                    ht = []
                    war = mo["t_y"][-1] if mo["t_y"] else None
                    for f in range(nf):
                        bk = bank[mo["h"] % 3]
                        mo["h"] += 1
                        wc = slice(128 * (e * nf + f), 128 * (e * nf + f) + 128)
                        yh = y_high[:, b % 2, 512 * (c % 2):512 * (c % 2) + 512]
                        yl = y_low[:, 512 * c:512 * c + 512]
                        for i, (wp, yp) in enumerate(((w_low[:, wc], yh), (w_hi[:, wc], yl), (w_hi[:, wc], yh))):
                            p = q.pe(lambda en, bk=bk, i=i, wp=wp, yp=yp: en.matmul(
                                bk.t[:, :], wp, yp, start=(i == 0), stop=(i == 2)), bk.free, t_w, t_zt)
                        k = (e % 2) * nf + f
                        kw = dict(bias=cols[:, 8 + e * nf + f:9 + e * nf + f]) if has_bias else {}
                        bk.free = q.act(lambda en, bk=bk, k=k, kw=kw: en.activation(PB[:, k, :], bk.t[:, :], func, **kw),
                                        p, war, t_cols)
                        ht.append(bk.free)
                        if f < nf - 1:
                            yield
                    if mo["prev"] is not None:
                        down(*mo["prev"])
                    mo["prev"] = (c, e, ht, nf, t_c)
                    yield
            if b == B - 1:
                down(*mo["prev"])
                mo["prev"] = None

        def dv(fn, *w):
            return q.dve(fn, *w)

        def g3(i, k, b):
            return gs[:, i, 0:NT * k].rearrange("p (t k) -> p t k", k=k)[:, 8 * b:8 * b + 8, :]

        def g1(i, b):
            return gs[:, i, 8 * b:8 * b + 8]

        def wide(ap, k):
            return ap.unsqueeze(2).broadcast_to((128, 8, k))

        def first_max(lgv, i, k, b, w):
            m, oh, c = g1(i + 1, b), g3(i, k, b), g1(i + 2, b)
            a1 = dv(lambda e: e.tensor_reduce(m, lgv, AX.X, ALU.max), w)
            a2 = dv(lambda e: e.tensor_tensor(oh, lgv, wide(m, k), ALU.is_equal), a1)
            a3 = dv(lambda e: e.tensor_tensor(oh, oh, idx[:, 0:k].unsqueeze(1).broadcast_to((128, 8, k)), ALU.mult), a2, t_idx)
            a4 = dv(lambda e: e.tensor_reduce(c, oh, AX.X, ALU.max), a3)
            return dv(lambda e: e.tensor_tensor(oh, oh, wide(c, k), ALU.is_equal), a4)

        def logits(b, wg, k, t_z, dst, b0):
            bk = misc()
            for j in range(8):
                t = 8 * b + j
                p = q.pe(lambda e, t=t, j=j, bk=bk: e.matmul(bk.t[:, k * j:k * j + k], ZT[:, 128 * t:128 * t + 128], wg,
                                                             start=True, stop=True), t_z, bk.free)
            bk.free = dv(lambda e, bk=bk: e.tensor_tensor(dst, bk.t[:, 0:8 * k].rearrange("p (t k) -> p t k", k=k),
                                                          gb[:, b0:b0 + k].unsqueeze(1).broadcast_to((128, 8, k)), ALU.add),
                         p, t_gb)
            return bk.free

        t_m0 = [load("m", W2[:, 0:2048], ins["L0w2"], ssm_done), load("m", b2s[:, :], ins["L0b2"]), t_w1]
        t_bc2 = load("bc2", bc[:, 0:1, :], ins["rows2"].partition_broadcast(128), ssm_bias)
        WL = WT[:, 576:1920]

        prep0 = Prep(0, WT[:, 0:128], WT[:, 128:256], WT[:, 256:384], cols[:, 4:5], cols[:, 5:6], bc[:, 1, :], None, t_w0)

        def norm_qkv(b, prep, w):
            z = []
            yield from ln(X, b, Z, z, w)
            yield
            t = transposed(Z, b, z, ZT)
            yield
            yield from prep.qkv(b, t)

        def norm2_qkv(b, w):
            z, z2 = [], []
            yield from ln(X, b, Z, z, w)
            yield from ln(Z, b, W, z2, z)
            yield
            t = transposed(W, b, z2, ZT, scale=cols[:, 24:25], bias=cols[:, 25:26])
            yield
            yield from preps[2].qkv(b, t)

        bkf = misc()
        p = q.pe(lambda e: e.matmul(bkf.t[:, 0:320], WL[:, 0:128], WL[:, 128:448], start=True, stop=True), t_wl, bkf.free)
        WF = WL[:, 896:1216]
        f1_ = q.act(lambda e: e.activation(WF, bkf.t[:, 0:320], ACT.Copy), p)
        bkf.free = f1_
        rp0, rp1 = WL[:, 1216:1280], WL[:, 1280:1344]
        f2 = [q.dve(lambda e: e.tensor_copy(rp0[:, 0:32], WL[:, 576:608]), t_wl),
              q.dve(lambda e: e.tensor_copy(rp0[:, 32:64], WF[:, 256:288]), f1_),
              q.dve(lambda e: e.tensor_copy(rp1[:, 0:32], WL[:, 608:640]), t_wl),
              q.dve(lambda e: e.tensor_copy(rp1[:, 32:64], WF[:, 288:320]), f1_)]
        lg = gs[:, 11:13, :].rearrange("p a b -> p (a b)")[:, 0:384].rearrange("p (t k) -> p t k", k=12)
        t_gate, t_yt, t_sp = {}, {}, {}

        def before0(b):
            yield from project(b, WT[:, 384:512], t_w0, Z, Z, 2)
            z = []
            yield from ln(Z, b, Z, z, proj[b])
            zs = Z[:, 8 * b:8 * b + 8, :]
            p1 = q.pool(lambda e: e.tensor_tensor(zs, zs, bc[:, 3:4, :].broadcast_to((128, 8, 128)), ALU.mult), z, t_bc)
            p2 = q.pool(lambda e: e.tensor_tensor(zs, zs, bc[:, 4:5, :].broadcast_to((128, 8, 128)), ALU.add), p1)
            for _ in range(5):
                yield
            t_yt[b] = transposed(Z, b, p2, ZT)
            yield
            lb = lg[:, 8 * b:8 * b + 8, :]
            a = logits(b, WT[:, 512:524], 12, t_yt[b], lb, 0)
            t_sp[b] = split_y(b, a)
            yield
            lgv = lb[:, :, 0:4]
            t_oh = first_max(lgv, 1, 4, b, a)
            gx, gsum = g3(4, 4, b), g1(5, b)
            a = dv(lambda e: e.tensor_tensor(gx, lgv, wide(g1(2, b), 4), ALU.subtract), t_oh)
            a_e = q.act(lambda e: e.activation(gx, gx, ACT.Exp), a)
            l0, l1 = lb[:, :, 4:8], lb[:, :, 8:12]
            em, x0, x1, f1, es = (g3(i, 4, b) for i in (6, 7, 8, 9, 10))
            b1 = dv(lambda e: e.tensor_tensor(em, l0, l1, ALU.max), a)
            b2 = dv(lambda e: e.tensor_tensor(x0, l0, em, ALU.subtract), b1)
            b3 = dv(lambda e: e.tensor_tensor(x1, l1, em, ALU.subtract), b1)
            b4 = q.act(lambda e: e.activation(x0, x0, ACT.Exp), b2)
            b5 = q.act(lambda e: e.activation(x1, x1, ACT.Exp), b3)
            b6 = dv(lambda e: e.tensor_tensor(f1, l1, l0, ALU.is_gt), a)
            a = dv(lambda e: e.tensor_reduce(gsum, gx, AX.X, ALU.add), a_e)
            b7 = dv(lambda e: e.tensor_tensor(es, x0, x1, ALU.add), b4, b5)
            yield
            b8 = dv(lambda e: e.tensor_tensor(es, es, wide(gsum, 4), ALU.mult), b7, a)
            b9 = dv(lambda e: e.reciprocal(es, es), b8)
            b10 = dv(lambda e: e.tensor_tensor(es, es, g3(1, 4, b), ALU.mult), b9)
            cc = gs[:, 0, :].rearrange("p (t g k) -> p t g k", g=4, k=2)[:, 8 * b:8 * b + 8]
            b11 = dv(lambda e: e.tensor_tensor(cc[:, :, :, 1], es, f1, ALU.mult), b10, b6)
            t_gate[b] = dv(lambda e: e.tensor_tensor(cc[:, :, :, 0], es, cc[:, :, :, 1], ALU.subtract), b11)
            yield

        rings = Rings(prep0)
        rings.fill(range(8), None)
        chain([norm_qkv(b, prep0, t_x[b]) for b in range(B - 1)])
        t_m0.append(split_w(2048, w_high0, q.pool, t_w1, ssm_done))
        rings.first(range(8))
        mb0 = before0(0)
        attention(rings, norm_qkv(B - 1, prep0, t_x[B - 1]), mb0, PIECES0)
        prep1 = Prep(1, WL[:, 448:576], WF[:, 0:128], WF[:, 128:256], cols[:, 6:7], cols[:, 6:7], None, (rp0, rp1),
                     [t_wl, f1_, f2, t_rt])
        rings = Rings(prep1)
        mo["t_y"].append(ended[-1][0])

        def after0(b):
            zs = Z[:, 8 * b:8 * b + 8, :]
            ws = W[:, 8 * b:8 * b + 8, :]
            xs = X[:, 8 * b:8 * b + 8, :]
            while mo["prev"] is not None and mo["prev"][0] <= 2 * b + 1:
                yield
            a = dv(lambda e: e.tensor_tensor(zs, zs, ws, ALU.add), [accs[(c, j)] for c in (2 * b, 2 * b + 1) for j in range(4)])
            yield
            z = []
            yield from ln(Z, b, Z, z, a)
            p1 = q.pool(lambda e: e.tensor_tensor(zs, zs, bc[:, 5:6, :].broadcast_to((128, 8, 128)), ALU.mult), z)
            p2 = q.pool(lambda e: e.tensor_tensor(xs, xs, zs, ALU.add), p1)
            p3 = q.pool(lambda e: e.tensor_tensor(xs, xs, bc[:, 0:1, :].broadcast_to((128, 8, 128)), ALU.add), p2, t_bc2)
            yield
            yield
            yield from norm_qkv(b, prep1, p3)

        def moe0(b):
            return moe(b, 2, ACT.Relu, w_high0, t_m0, t_gate[b], t_sp[b], True)

        run(mb0)
        rate = RATE0
        merge(moe0(0), before0(1), rate)
        merge(moe0(1), before0(2), rate, after0(0))
        rings.fill([0, 1, 2], ended[-1])
        merge(moe0(2), before0(3), rate, after0(1))

        def moe0_and_first():
            for i, _ in enumerate(moe0(3)):
                if i == 8:
                    rings.first([0, 1, 2])
                yield

        merge(moe0_and_first(), None, rate, after0(2))
        rings.fill([3, 4, 5], [ended[-1], mo["t_y"][-1]])
        rings.late = [3, 4, 5]
        side = chained([g for g, _ in back])
        back.clear()
        def between(b):
            yield from project(b, WL[:, 640:768], t_wl, X, X, None)
            yield from norm2_qkv(b, proj[b])

        t_w3 = load("w3", WT[:, 0:520], ins["w_l2"], mo["t_y"][-1])
        spread = after0(B - 1)
        then = [between(b) for b in range(B - 1)]

        def enter2():
            run(spread)
            preps[2] = Prep(2, WT[:, 0:128], WT[:, 128:256], WT[:, 256:384], cols[:, 6:7], cols[:, 6:7], None, None, t_w3)
            preps[2].slot_done = [prep1.slot_done, prep1.slot_done]

        start = [24 + 14 + 24 * 8 * (b + 1) + 12 for b in range(B - 1)]
        rings1, rings2 = rings, []

        def early():
            rings2.append(Rings(preps[2]))
            rings2[0].fill(range(4), [rings1.mained[60], rings1.mained[61]])
            rings2[0].first(range(4))

        attention(rings, side, then, 0, spread, start, [(start[0] - 1, enter2), (24 + 14 + 24 * 31 + 3, early)])
        for g in then:
            run(g)
        prep2 = preps[2]
        t_m3 = [load("m", W2[:, :], ins["L1w2"], ended[-1])]
        rings = rings2[0]
        rings.fill(range(4, 8), ended[-1])
        rings.late = range(4, 8)

        t_xr, t_od = {}, []
        od = out.rearrange("(t p) d -> p t d", p=128)

        def before1(b):
            yield from project(b, WT[:, 384:512], t_w3, Z, Z, None)
            z = []
            yield from ln(Z, b, W, z, proj[b])
            zs, xs = Z[:, 8 * b:8 * b + 8, :], X[:, 8 * b:8 * b + 8, :]
            t_xr[b] = q.pool(lambda e: e.tensor_tensor(xs, xs, zs, ALU.add), proj[b])
            yield
            yield
            yield
            t_yt[b] = transposed(W, b, z, ZT, scale=cols[:, 26:27], bias=cols[:, 27:28])
            yield
            l8 = g3(7, 8, b)
            a = logits(b, WT[:, 512:520], 8, t_yt[b], l8, 12)
            t_sp[b] = split_y(b, a)
            yield
            t_oh = first_max(l8, 1, 8, b, a)
            t_gate[b] = dv(lambda e: e.tensor_copy(g3(0, 8, b), g3(1, 8, b)), t_oh)
            yield

        mb1 = before1(0)

        def enter3():
            t_m3.append(load("m", W1[:, :], ins["L1w1"], prep2.slot_done))

        attention(rings, between(B - 1), mb1, PIECES2, None, None, [(300, enter3)])
        mo["t_y"].append(ended[-1][0])
        t_m3.append(split_w(4096, w_high3, q.dve, t_m3[1], ended[-1]))

        def after1(b):
            while mo["prev"] is not None and mo["prev"][0] <= 2 * b + 1:
                yield
            for c in (2 * b, 2 * b + 1):
                xs = X[:, 4 * c:4 * c + 4, :]
                a = dv(lambda e, xs=xs, c=c: e.tensor_tensor(xs, xs, W[:, 4 * c:4 * c + 4, :], ALU.add),
                       [accs[(c, j)] for j in range(4)], t_xr[b])
                q.dma("o", od[:, 4 * c:4 * c + 4, :], xs, a)
                yield

        def moe1(b):
            return moe(b, 4, ACT.Gelu_apprx_tanh, w_high3, t_m3, t_gate[b], t_sp[b], False)

        run(mb1)
        rate = RATE1
        merge(moe1(0), before1(1), rate)
        merge(moe1(1), before1(2), rate, after1(0))
        merge(moe1(2), before1(3), rate, after1(1))
        merge(moe1(3), None, rate, after1(2))
        run(after1(3))
        q.finish([t for t in q.dma_open])
        block = ctx.enter_context(nc.Block())
        q.emit(block)


def kernel(**I):
    import numpy as _np
    import ml_dtypes
    import concourse.bacc as _bacc
    from concourse import mybir as _mybir
    from concourse.bass_utils import run_bass_kernel_spmd as _run

    f32 = _np.float32
    I = {k: _np.asarray(v) for k, v in I.items()}

    def chunks(a):
        n = a.shape[0] // 128
        return _np.concatenate([a[128 * c:128 * c + 128] for c in range(n)], axis=1)

    def rep4(a):
        z = _np.zeros((a.shape[0], 16), f32)
        return _np.concatenate([a, z] * 4, axis=1)

    def swap(a):
        return _np.concatenate([a[:, 16:32], a[:, 0:16]], axis=1)

    eye = _np.eye(128, dtype=f32)
    z1 = _np.zeros((128, 1), f32)
    cols = [I["L0_attn_norm_w"][:, None], I["L0_attn_norm_b"][:, None],
            I["L0_attn_b_in"][0:128, None], I["L0_attn_b_in"][128:256, None],
            I["L0_ffn_in_proj_b"][0:128, None], I["L0_ffn_in_proj_b"][128:256, None], z1, z1,
            I["L0_ffn_b1"].reshape(16, 128).T,
            I["L1_ffn_ln1_w"][:, None], I["L1_ffn_ln1_b"][:, None], I["L1_ffn_ln2_w"][:, None], I["L1_ffn_ln2_b"][:, None]]
    cols = _np.concatenate(cols, axis=1)
    cols = _np.concatenate([cols, _np.zeros((128, 40 - cols.shape[1]), f32)], axis=1)
    rows = _np.stack([I["L0_attn_b_out"], I["L0_ffn_in_proj_b"][256:384], I["L0_ffn_out_proj_b"],
                      I["L0_ffn_ln1_g"], I["L0_ffn_ln1_b"], I["L0_ffn_ln2_g"]])
    kk, qq = _np.meshgrid(_np.arange(128), _np.arange(128), indexing="ij")
    m_max = _np.where(qq > kk, NEG, 0.0)
    m_main = _np.where(kk > qq, NEG, 0.0)
    mask = _np.concatenate([m_max, m_main], axis=1).astype(ml_dtypes.bfloat16)
    w_ssm = _np.concatenate([chunks(I["L0_attn_W_in"]), chunks(rep4(I["L0_attn_A"])), chunks(rep4(I["L0_attn_B_ssm"])),
                             chunks(rep4(I["L0_attn_C_ssm"])), chunks(I["L0_attn_W_out"].T)], axis=1)
    w_l0 = _np.concatenate([I["L0_ffn_in_proj_w"].T, I["L0_ffn_out_proj_w"].T, I["L0_ffn_w_group"],
                            I["L0_ffn_w_expert"][:, :, 0].T, I["L0_ffn_w_expert"][:, :, 1].T,
                            ], axis=1)
    w_l1 = _np.concatenate([I["L1_attn_W_kv_down"].T, I["L1_attn_W_k_up"], I["L1_attn_W_v_up"], I["L1_attn_W_k_rope"],
                            swap(I["L1_attn_W_k_rope"]), I["L1_attn_W_q"], I["L1_attn_W_q_rope"],
                            swap(I["L1_attn_W_q_rope"]), I["L1_attn_W_o"], _np.zeros((128, 128), f32)], axis=1)
    w_l2 = _np.concatenate([I["L1_ffn_w_qkv"], I["L1_ffn_w_proj"], I["L1_ffn_gate_w"]], axis=1)
    inv = (f32(1.0) / _np.power(f32(10000.0), _np.arange(0, 32, 2, dtype=f32) / f32(32))).astype(f32)
    fr = _np.outer(_np.arange(S, dtype=f32), inv).astype(f32).T
    cs, sn = _np.cos(fr), _np.sin(fr)
    rope = _np.concatenate([_np.concatenate([cs, cs, cs, cs]), _np.concatenate([-sn, sn, -sn, sn])], axis=1).astype(f32)
    fill = _np.zeros((56, 4, 4, 1024), ml_dtypes.bfloat16)
    fill[24:27, :, 1::2, :] = 1.0
    fill = fill.reshape(56, 16384)
    be = I["L0_ffn_b_expert"]
    arrays = {
        "x": I["L0_attn_x"].reshape(B * S, D), "cols": cols, "rows": rows, "rows2": I["L0_ffn_ln2_b"][None, :],
        "identf": eye, "identb": eye.astype(ml_dtypes.bfloat16), "maskb": mask,
        "fill": fill,
        "idx": _np.arange(8, 0, -1).astype(f32),
        "gate_b": _np.concatenate([I["L0_ffn_b_group"], be[:, 0], be[:, 1], I["L1_ffn_gate_b"]]),
        "w_ssm": w_ssm, "w_l0": w_l0, "w_l1": w_l1, "w_l2": w_l2, "rope": rope,
        "L0w1": I["L0_ffn_w1"].transpose(1, 0, 2).reshape(128, 2048),
        "L0w2": I["L0_ffn_w2"].reshape(8, 2, 128, 128).transpose(2, 0, 1, 3).reshape(128, 2048),
        "L0b2": I["L0_ffn_b2"],
        "L1w1": I["L1_ffn_w1"].transpose(1, 0, 2).reshape(128, 4096),
        "L1w2": I["L1_ffn_w2"].reshape(8, 4, 128, 128).transpose(2, 0, 1, 3).reshape(128, 4096),
    }
    nc = _bacc.Bacc("TRN2", target_bir_lowering=False, num_devices=1)
    feed, aps = {}, {}
    for name, a in arrays.items():
        a = _np.ascontiguousarray(a)
        feed[f"in_{name}"] = a
        aps[name] = nc.dram_tensor(f"in_{name}", a.shape, _mybir.dt.from_np(a.dtype), kind="ExternalInput").ap()
    out = nc.dram_tensor("out_0", (B * S, D), F32, kind="ExternalOutput").ap()
    build(nc, aps, out)
    r = _run(nc, [feed], core_ids=[0])
    return r.results[0]["out_0"].reshape(B, S, D)
```
